# Optimizing a Trainium2 kernel written in Bass

```python
import numpy as np
import jax
import jax.numpy as jnp

def _softmax(x, axis=-1):
    return jax.nn.softmax(x, axis=axis)

def _gelu(x):
    return jax.nn.gelu(x, approximate=True)

def _silu(x):
    return jax.nn.silu(x)

def _sigmoid(x):
    return jax.nn.sigmoid(x)

def _layernorm(x, axis=-1, eps=1e-05):
    m = jnp.mean(x, axis=axis, keepdims=True)
    v = jnp.var(x, axis=axis, keepdims=True)
    return (x - m) / jnp.sqrt(v + eps)

def _scatter_add(tgt, idx, src, axis=0):
    return tgt.at[idx].add(src)

def _segment_sum(src, seg, n):
    return jax.ops.segment_sum(src, seg, n)
kernel_name = 'mk_xattn_ffn_d2_seqx_r8_0f651b'

def setup_inputs(seed: int=0):
    np.random.seed(seed)
    _w = jnp.asarray

    def _rec_inputs():
        import jax
        import jax.numpy as jnp
        _rk = jax.random.key(seed)
        x = 4.136e-05 + 0.9999 * jax.random.normal(jax.random.fold_in(_rk, 1), (4, 256, 256), jnp.float32)
        _lenS = 256 - jax.random.randint(jax.random.fold_in(_rk, 7), (4,), 0, max(1, 256 // 4) + 1, jnp.int32)
        _lenS2 = 256 - jax.random.randint(jax.random.fold_in(_rk, 8), (4,), 0, max(1, 256 // 4) + 1, jnp.int32)
        _ctx_1024P = jax.random.normal(jax.random.fold_in(_rk, 11), (4, 16, 128), jnp.float32)
        _ctx_1024c = jax.random.dirichlet(jax.random.fold_in(_rk, 511), 0.3 * jnp.ones((16,), jnp.float32), (4, 256))
        _ctx_1024t = jnp.einsum('bsk,bkd->bsd', _ctx_1024c, _ctx_1024P)
        _ctx_1024t = _ctx_1024t * jax.lax.rsqrt(jnp.mean(jnp.square(_ctx_1024t)) + 1e-12) * 0.953939
        ctx_1024 = -0.000292821 + 1.00034 * (_ctx_1024t + 0.3 * jax.random.normal(jax.random.fold_in(_rk, 611), (4, 256, 128), jnp.float32))
        return (x, ctx_1024)
    x, ctx_1024 = _rec_inputs()

    def _L0_xattn_setup():
        import jax, jax.numpy as jnp
        import numpy as np
        import math
        B, L, DM = (2, 256, 128)
        DS, DC, EXP = (16, 4, 2)
        DI = EXP * DM
        DR = math.ceil(DM / 16)
        DT_MIN, DT_MAX, DT_FLOOR = (0.001, 0.1, 0.0001)

        def _ssm_forward(hidden_states, z, in_proj_w, conv_w, conv_b, x_proj_w, dt_proj_w, dt_proj_b, A_log, D):
            b = hidden_states.shape[0]
            x = jnp.einsum('ed,bld->bel', in_proj_w, hidden_states)
            xp = jnp.pad(x, ((0, 0), (0, 0), (DC - 1, 0)))
            xc = jax.lax.conv_general_dilated(xp, conv_w[:, None, :], window_strides=(1,), padding='VALID', dimension_numbers=('NCH', 'OIH', 'NCH'), feature_group_count=DI)
            u = jax.nn.silu(xc + conv_b[None, :, None])
            x_dbl = jnp.einsum('ke,bel->bkl', x_proj_w, u)
            dt_lo = x_dbl[:, :DR]
            Bm = x_dbl[:, DR:DR + DS]
            Cm = x_dbl[:, DR + DS:]
            delta = jax.nn.softplus(jnp.einsum('er,brl->bel', dt_proj_w, dt_lo) + dt_proj_b[None, :, None])
            A = -jnp.exp(A_log)

            def step(state, xs):
                d_t, B_t, C_t, u_t = xs
                dA = jnp.exp(d_t[..., None] * A)
                state = state * dA + (d_t * u_t)[..., None] * B_t[:, None, :]
                y_t = jnp.einsum('ben,bn->be', state, C_t)
                return (state, y_t)
            xs = (jnp.moveaxis(delta, -1, 0), jnp.moveaxis(Bm, -1, 0), jnp.moveaxis(Cm, -1, 0), jnp.moveaxis(u, -1, 0))
            state0 = jnp.zeros((b, DI, DS), delta.dtype)
            _, ys = jax.lax.scan(step, state0, xs)
            y = jnp.moveaxis(ys, 0, -1)
            y = y + D[None, :, None] * u
            y = y * jax.nn.silu(z)
            return jnp.swapaxes(y, 1, 2)
        key = jax.random.key(seed)
        ks = jax.random.split(key, 8)
        hidden_states = jax.random.normal(ks[0], (B, L, DM), jnp.float32)
        z = jax.random.normal(ks[1], (B, DI, L), jnp.float32)
        in_proj_w = jax.random.normal(ks[2], (DI, DM), jnp.float32) * DM ** (-0.5)
        conv_w = jax.random.normal(ks[3], (DI, DC), jnp.float32) * DC ** (-0.5)
        conv_b = jnp.zeros((DI,), jnp.float32)
        x_proj_w = jax.random.normal(ks[4], (DR + 2 * DS, DI), jnp.float32) * DI ** (-0.5)
        dt_std = DR ** (-0.5)
        dt_proj_w = jax.random.uniform(ks[5], (DI, DR), jnp.float32, -dt_std, dt_std)
        dt = jnp.exp(jax.random.uniform(ks[6], (DI,), jnp.float32) * (math.log(DT_MAX) - math.log(DT_MIN)) + math.log(DT_MIN))
        dt = jnp.clip(dt, DT_FLOOR)
        dt_proj_b = dt + jnp.log(-jnp.expm1(-dt))
        A_log = jnp.log(jnp.broadcast_to(jnp.arange(1, DS + 1, dtype=jnp.float32), (DI, DS)))
        D = jnp.ones((DI,), jnp.float32)
        return dict(hidden_states=hidden_states, z=z, in_proj_w=in_proj_w, conv_w=conv_w, conv_b=conv_b, x_proj_w=x_proj_w, dt_proj_w=dt_proj_w, dt_proj_b=dt_proj_b, A_log=A_log, D=D)
    _L0_xattn_all = _L0_xattn_setup()
    _L0_xattn_in = {k: v for k, v in _L0_xattn_all.items() if k in ('in_proj_w', 'conv_w', 'conv_b', 'x_proj_w', 'dt_proj_w', 'dt_proj_b', 'A_log', 'D')}
    del _L0_xattn_all

    def _L0_ffn_setup():
        import jax, jax.numpy as jnp
        import numpy as np
        TOP_K = 2
        EPS = 1e-06
        key = jax.random.key(seed)
        ks = jax.random.split(key, 5)
        B, S, D, E = (4, 256, 256, 8)
        sd = 1.0 / np.sqrt(D)
        return {'x': jax.random.normal(ks[0], (B, S, D), jnp.float32), 'router_w': jax.random.normal(ks[1], (D, E), jnp.float32) * sd, 'router_b': jnp.zeros((E,), jnp.float32), 'expert_w': jax.random.normal(ks[2], (E, D, D), jnp.float32) * sd, 'expert_b': jnp.zeros((E, D), jnp.float32), 'proj_w': jax.random.normal(ks[3], (D, D), jnp.float32) * sd, 'proj_b': jnp.zeros((D,), jnp.float32), 'norm_w': jnp.ones((D,), jnp.float32)}
    _L0_ffn_all = _L0_ffn_setup()
    _L0_ffn_in = {k: v for k, v in _L0_ffn_all.items() if k in ('router_w', 'router_b', 'expert_w', 'expert_b', 'proj_w', 'proj_b', 'norm_w')}
    del _L0_ffn_all

    def _L1_xattn_setup():
        import jax, jax.numpy as jnp
        import numpy as np
        key = jax.random.key(seed)
        ks = jax.random.split(key, 6)
        B, L, N, C, D = (8, 64, 256, 128, 128)
        return {'teacher_logits': jax.random.normal(ks[0], (B, L, N), dtype=jnp.float32), 'teacher_features': jax.random.normal(ks[1], (B, N, C), dtype=jnp.float32), 'Wq': jax.random.normal(ks[2], (D, C), dtype=jnp.float32) * (1.0 / np.sqrt(C)), 'bq': jnp.zeros((D,), dtype=jnp.float32), 'Wk': jax.random.normal(ks[3], (D, C), dtype=jnp.float32) * (1.0 / np.sqrt(C)), 'bk': jnp.zeros((D,), dtype=jnp.float32)}
    _L1_xattn_all = _L1_xattn_setup()
    _L1_xattn_in = {k: v for k, v in _L1_xattn_all.items() if k in ('Wq', 'bq', 'Wk', 'bk')}
    del _L1_xattn_all

    def _L1_ffn_setup():
        import jax, jax.numpy as jnp
        import numpy as np
        B, S, D, K, R = (4, 256, 256, 8, 64)
        key = jax.random.key(seed)
        ks = jax.random.split(key, 7)
        x = jax.random.normal(ks[0], (B, S, D), dtype=jnp.float32)
        U = jax.random.normal(ks[1], (K, D, R), dtype=jnp.float32) * 0.02
        V = jax.random.normal(ks[2], (K, R, D), dtype=jnp.float32) * 0.02
        W1 = jax.random.normal(ks[3], (D, D), dtype=jnp.float32) * 0.02
        b1 = jnp.zeros((D,), dtype=jnp.float32)
        W2 = jax.random.normal(ks[4], (D, K), dtype=jnp.float32) * 0.02
        b2 = jnp.zeros((K,), dtype=jnp.float32)
        return {'x': x, 'U': U, 'V': V, 'W1': W1, 'b1': b1, 'W2': W2, 'b2': b2}
    _L1_ffn_all = _L1_ffn_setup()
    _L1_ffn_in = {k: v for k, v in _L1_ffn_all.items() if k in ('U', 'V', 'W1', 'b1', 'W2', 'b2')}
    del _L1_ffn_all
    return {'x': x, 'ctx_1024': ctx_1024, 'L0_xattn_in_proj_w': _L0_xattn_in['in_proj_w'], 'L0_xattn_conv_w': _L0_xattn_in['conv_w'], 'L0_xattn_conv_b': _L0_xattn_in['conv_b'], 'L0_xattn_x_proj_w': _L0_xattn_in['x_proj_w'], 'L0_xattn_dt_proj_w': _L0_xattn_in['dt_proj_w'], 'L0_xattn_dt_proj_b': _L0_xattn_in['dt_proj_b'], 'L0_xattn_A_log': _L0_xattn_in['A_log'], 'L0_xattn_D': _L0_xattn_in['D'], 'L0_ffn_router_w': _L0_ffn_in['router_w'], 'L0_ffn_router_b': _L0_ffn_in['router_b'], 'L0_ffn_expert_w': _L0_ffn_in['expert_w'], 'L0_ffn_expert_b': _L0_ffn_in['expert_b'], 'L0_ffn_proj_w': _L0_ffn_in['proj_w'], 'L0_ffn_proj_b': _L0_ffn_in['proj_b'], 'L0_ffn_norm_w': _L0_ffn_in['norm_w'], 'L1_xattn_Wq': _L1_xattn_in['Wq'], 'L1_xattn_bq': _L1_xattn_in['bq'], 'L1_xattn_Wk': _L1_xattn_in['Wk'], 'L1_xattn_bk': _L1_xattn_in['bk'], 'L1_ffn_U': _L1_ffn_in['U'], 'L1_ffn_V': _L1_ffn_in['V'], 'L1_ffn_W1': _L1_ffn_in['W1'], 'L1_ffn_b1': _L1_ffn_in['b1'], 'L1_ffn_W2': _L1_ffn_in['W2'], 'L1_ffn_b2': _L1_ffn_in['b2']}

def reference(x, ctx_1024, L0_xattn_in_proj_w, L0_xattn_conv_w, L0_xattn_conv_b, L0_xattn_x_proj_w, L0_xattn_dt_proj_w, L0_xattn_dt_proj_b, L0_xattn_A_log, L0_xattn_D, L0_ffn_router_w, L0_ffn_router_b, L0_ffn_expert_w, L0_ffn_expert_b, L0_ffn_proj_w, L0_ffn_proj_b, L0_ffn_norm_w, L1_xattn_Wq, L1_xattn_bq, L1_xattn_Wk, L1_xattn_bk, L1_ffn_U, L1_ffn_V, L1_ffn_W1, L1_ffn_b1, L1_ffn_W2, L1_ffn_b2):
    import jax
    import jax.numpy as jnp

    def _L0_xattn_ref(hidden_states, z, in_proj_w, conv_w, conv_b, x_proj_w, dt_proj_w, dt_proj_b, A_log, D):
        import jax, jax.numpy as jnp
        import numpy as np
        import math
        B, L, DM = (2, 256, 128)
        DS, DC, EXP = (16, 4, 2)
        DI = EXP * DM
        DR = math.ceil(DM / 16)
        DT_MIN, DT_MAX, DT_FLOOR = (0.001, 0.1, 0.0001)

        def _ssm_forward(hidden_states, z, in_proj_w, conv_w, conv_b, x_proj_w, dt_proj_w, dt_proj_b, A_log, D):
            b = hidden_states.shape[0]
            x = jnp.einsum('ed,bld->bel', in_proj_w, hidden_states)
            xp = jnp.pad(x, ((0, 0), (0, 0), (DC - 1, 0)))
            xc = jax.lax.conv_general_dilated(xp, conv_w[:, None, :], window_strides=(1,), padding='VALID', dimension_numbers=('NCH', 'OIH', 'NCH'), feature_group_count=DI)
            u = jax.nn.silu(xc + conv_b[None, :, None])
            x_dbl = jnp.einsum('ke,bel->bkl', x_proj_w, u)
            dt_lo = x_dbl[:, :DR]
            Bm = x_dbl[:, DR:DR + DS]
            Cm = x_dbl[:, DR + DS:]
            delta = jax.nn.softplus(jnp.einsum('er,brl->bel', dt_proj_w, dt_lo) + dt_proj_b[None, :, None])
            A = -jnp.exp(A_log)

            def step(state, xs):
                d_t, B_t, C_t, u_t = xs
                dA = jnp.exp(d_t[..., None] * A)
                state = state * dA + (d_t * u_t)[..., None] * B_t[:, None, :]
                y_t = jnp.einsum('ben,bn->be', state, C_t)
                return (state, y_t)
            xs = (jnp.moveaxis(delta, -1, 0), jnp.moveaxis(Bm, -1, 0), jnp.moveaxis(Cm, -1, 0), jnp.moveaxis(u, -1, 0))
            state0 = jnp.zeros((b, DI, DS), delta.dtype)
            _, ys = jax.lax.scan(step, state0, xs)
            y = jnp.moveaxis(ys, 0, -1)
            y = y + D[None, :, None] * u
            y = y * jax.nn.silu(z)
            return jnp.swapaxes(y, 1, 2)
        return _ssm_forward(hidden_states, z, in_proj_w, conv_w, conv_b, x_proj_w, dt_proj_w, dt_proj_b, A_log, D)

    def _L0_ffn_ref(x, router_w, router_b, expert_w, expert_b, proj_w, proj_b, norm_w):
        import jax, jax.numpy as jnp
        import numpy as np
        TOP_K = 2
        EPS = 1e-06
        B, S, D = x.shape
        E = router_b.shape[0]
        logits = jnp.einsum('bsd,de->bse', x, router_w) + router_b
        topk_vals, topk_idx = jax.lax.top_k(logits, TOP_K)
        topk_w = jax.nn.softmax(topk_vals, axis=-1)
        full_w = jnp.sum(jax.nn.one_hot(topk_idx, E, dtype=x.dtype) * topk_w[..., None], axis=-2)
        xf = x.reshape(-1, D)
        h = jnp.einsum('td,edf->etf', xf, expert_w) + expert_b[:, None, :]
        expert_out = jax.nn.silu(h)
        combined = jnp.einsum('etf,te->tf', expert_out, full_w.reshape(-1, E)).reshape(B, S, D)
        out = jnp.einsum('bsd,df->bsf', combined, proj_w) + proj_b
        y = x + out
        rms = jnp.sqrt(jnp.mean(y * y, axis=-1, keepdims=True) + EPS)
        return norm_w * (y / rms)

    def _L1_xattn_ref(teacher_logits, teacher_features, Wq, bq, Wk, bk):
        import jax, jax.numpy as jnp
        import numpy as np
        query = jnp.einsum('bnc,dc->bnd', teacher_features, Wq) + bq
        key = jnp.einsum('bnc,dc->bnd', teacher_features, Wk) + bk
        energy = jnp.einsum('bnd,bmd->bnm', query, key)
        attention = jax.nn.softmax(energy, axis=-1)
        x_m = jnp.einsum('bln,bmn->blm', teacher_logits, attention)
        return x_m

    def _L1_ffn_ref(x, U, V, W1, b1, W2, b2):
        import jax, jax.numpy as jnp
        import numpy as np
        B, S, D, K, R = (4, 256, 256, 8, 64)
        h = jax.nn.relu(jnp.einsum('bsd,de->bse', x, W1) + b1)
        alpha = jax.nn.softmax(jnp.einsum('bse,ek->bsk', h, W2) + b2, axis=-1)
        vx = jnp.einsum('krd,bsd->bskr', V, x)
        uvx = jnp.einsum('kdr,bskr->bskd', U, vx)
        out = jnp.einsum('bsk,bskd->bsd', alpha, uvx)
        return out
    x = x + _L0_xattn_ref(ctx_1024, _layernorm(x, axis=-1), L0_xattn_in_proj_w, L0_xattn_conv_w, L0_xattn_conv_b, L0_xattn_x_proj_w, L0_xattn_dt_proj_w, L0_xattn_dt_proj_b, L0_xattn_A_log, L0_xattn_D)
    x = x + _L0_ffn_ref(_layernorm(x, axis=-1), L0_ffn_router_w, L0_ffn_router_b, L0_ffn_expert_w, L0_ffn_expert_b, L0_ffn_proj_w, L0_ffn_proj_b, L0_ffn_norm_w)
    x = x + _L1_xattn_ref(_layernorm(x, axis=-1), ctx_1024, L1_xattn_Wq, L1_xattn_bq, L1_xattn_Wk, L1_xattn_bk)
    x = x + _L1_ffn_ref(_layernorm(x, axis=-1), L1_ffn_U, L1_ffn_V, L1_ffn_W1, L1_ffn_b1, L1_ffn_W2, L1_ffn_b2)
    return x

_drawn_inputs = setup_inputs


def setup_inputs(seed=0):
    import zlib

    import numpy as np

    out = dict(_drawn_inputs(seed))
    spreads = {'L0_xattn_conv_b': (0.0, 0.1),
     'L0_xattn_D': (1.0, 0.2),
     'L0_ffn_router_b': (0.0, 0.1),
     'L0_ffn_expert_b': (0.0, 0.374),
     'L0_ffn_proj_b': (0.0, 0.1),
     'L0_ffn_norm_w': (1.0, 0.2),
     'L1_xattn_bq': (0.0, 0.1),
     'L1_xattn_bk': (0.0, 0.8),
     'L1_ffn_b1': (0.0, 0.8),
     'L1_ffn_b2': (0.0, 0.8)}
    factors = {'L0_xattn_dt_proj_w': 3.953,
     'L1_ffn_U': 6.902,
     'L1_ffn_V': 6.911,
     'L1_ffn_W1': 8.0,
     'L1_ffn_W2': 8.0}
    for name, (base, spread) in spreads.items():
        noise = np.random.default_rng([zlib.crc32(name.encode()), seed]).standard_normal(out[name].shape)
        drawn = base * np.exp(spread * noise) if base else spread * noise
        out[name] = jnp.asarray(drawn.astype(out[name].dtype))
    for name, factor in factors.items():
        out[name] = (out[name] * factor).astype(out[name].dtype)
    return out
```

```python
import concourse.bass as bass
from concourse import mybir
from contextlib import ExitStack

F32 = mybir.dt.float32
F32R = mybir.dt.float32r
U32 = mybir.dt.uint32
ALU = mybir.AluOpType
ACT = mybir.ActivationFunctionType
AX = mybir.AxisListType

P = 128
B, L, D, C = 4, 256, 256, 128
H = D // P
DS, DC, DR = 16, 4, 8
E = 8
K, R = 8, 64
KT = K * R // P
CHUNKS = H * E // 2
SLOTS = 2 * DS

EARLY = [("in_projT", D), ("conv_w", DC * D), ("conv_b", H), ("x_projT", H * (DR + 2 * DS)), ("dt_b", H),
         ("Dskip", H), ("A_log", H * DS), ("ident", P)]
LATE = [("WqT", P), ("WkT", P), ("bq", 1), ("bk", 1), ("router", H * E), ("router_b", E), ("proj", H * D),
        ("proj_b", D), ("norm_w", D), ("W1", H * D), ("b1", H), ("W2", H * K), ("b2", K), ("VT", H * K * R),
        ("UT", KT * D), ("iota", E)]


class Signal:

    def __init__(self, handle, per=1):
        self.sem, self.per = handle, per

    def value(self, b, k=None):
        return self.per * b + (self.per if k is None else k)


def wait(engine, signal, b, k=None):
    if b >= 0:
        engine.wait_ge(signal.sem, signal.value(b, k))


def build(nc, early, late, experts, expert_b, rowsel, dt_projT, ctxT, x, out):
    with ExitStack() as stack:
        def sb(name, shape, dt=F32):
            return stack.enter_context(nc.sbuf_tensor(name, shape, dt))

        def ps(name):
            return stack.enter_context(nc.psum_tensor(name, [P, 512], F32))

        def sem(name):
            return stack.enter_context(nc.semaphore(name))

        def sig(name, per=1):
            return Signal(sem(name), per)

        def halves(t):
            return t.rearrange("p (h c) -> p h c", h=H)

        early_sb = sb("early_sb", [P, sum(n for _, n in EARLY)])
        late_sb = sb("late_sb", [P, sum(n for _, n in LATE)])
        cst = {}
        for tile, table in ((early_sb, EARLY), (late_sb, LATE)):
            at = 0
            for name, n in table:
                cst[name] = tile[:, at:at + n]
                at += n
        ident = cst["ident"]
        xproj = halves(cst["x_projT"])
        dtp = sb("dtp", [DR, D])
        ew_hi = sb("ew_hi", [P, H, E * D], F32R)
        ew_lo = sb("ew_lo", [P, H, E * D], F32R)
        rw_hi = sb("rw_hi", [P, H, E], F32R)
        rw_lo = sb("rw_lo", [P, H, E], F32R)
        eb_rows = sb("eb_rows", [2, E * D], F32R)
        sel_sb = sb("sel_sb", [2, 2])
        ones2 = sb("ones2", [2, P])
        ones2r = sb("ones2r", [2, P], F32R)
        negA = sb("negA", [P, H * DS])
        negA_n = sb("negA_n", [P, H * DS])
        half_cb = sb("half_cb", [P, H])
        diagD = sb("diagD", [P, H, P])
        half_ident = sb("half_ident", [P, P])
        neg_half = sb("neg_half", [P, H])
        ctx = sb("ctx", [P, B, DC - 1 + L])
        xin = sb("xin", [P, B, H, D])
        gst = sb("gst", [P, H, 6])
        gmv = sb("gmv", [P, H, 2])
        gve = sb("gve", [P, H])
        grstd = sb("grstd", [P, H])
        zn = sb("zn", [P, H, L])
        gate = sb("gate", [P, 2, H, D])
        uth = sb("uth", [P, H, L])
        zth = uth
        uhalf = sb("uhalf", [P, H, L])
        u = sb("u", [P, H, L])
        dtB = sb("dtB", [DR + DS, L])
        Ct = sb("Ct", [P, 2, H, DS])
        sp_abs = sb("sp_abs", [P, H, L])
        sp_exp = sp_log = sp_abs
        sp_pos = uhalf
        delta = sb("delta", [P, 2, H, L])
        du = sb("du", [P, 2, H, L])
        Brep = sb("Brep", [P, 2, DS * L])
        y = sb("y", [P, 2, H, D])
        qT = sb("qT", [P, L])
        kT = sb("kT", [P, L])
        amax = sb("amax", [P, H])
        aexp = sb("aexp", [P, H, L])
        asum = sb("asum", [P, H])
        arec = sb("arec", [P, H])
        att = aexp
        attT = sb("attT", [P, 3, H, L])
        dBu = sb("dBu", [P, 2, H, L])
        hst = sb("hst", [P, 2, H, L])
        x1 = sb("x1", [P, 2, H, D])
        mst = sb("mst", [P, H, 6])
        mmv = sb("mmv", [P, H, 2])
        mve = sb("mve", [P, H])
        mrstd = sb("mrstd", [P, H])
        xn1 = sb("xn1", [P, H, D])
        xn1b = sb("xn1b", [P, 2, H, D])
        xh = sb("xh", [P, H, L], F32R)
        xl = sb("xl", [P, H, L], F32R)
        logit = sb("logit", [P, H, E])
        top = sb("top", [P, H, 8])
        topi = sb("topi", [P, H, 8], U32)
        topf = sb("topf", [P, H, 8])
        gap = sb("gap", [P, H])
        gexp = sb("gexp", [P, H])
        gden = sb("gden", [P, H])
        w0 = sb("w0", [P, H])
        w1 = sb("w1", [P, H])
        pick0 = sb("pick0", [P, H, E])
        pick1 = sb("pick1", [P, H, E])
        wfull = sb("wfull", [P, H, E])
        diagw = sb("diagw", [P, H, E, P])
        eth = sb("eth", [P, 2, 512])
        eg = eth
        comb = sb("comb", [P, H, L])
        yss = sb("yss", [P, H])
        yve = sb("yve", [P, H])
        yrms = sb("yrms", [P, H])
        ynw = sb("ynw", [P, H, D])
        ysq = ynw
        x2 = sb("x2", [P, H, D])
        x3 = sb("x3", [P, H, D])
        tst = sb("tst", [P, 2, H, 6])
        tmv = sb("tmv", [P, 2, H, 2])
        tve = sb("tve", [P, 2, H])
        trstd = sb("trstd", [P, 2, H])
        xn2 = sb("xn2", [P, H, D])
        xn2T = sb("xn2T", [P, H, L])
        xn3, xn3T = xn2, xn2T
        h1 = ynw
        lg2 = sb("lg2", [P, H, K])
        lmax = sb("lmax", [P, H])
        alpha = sb("alpha", [P, H, K])
        lsum = sb("lsum", [P, H])
        lrec = sb("lrec", [P, H])
        avx = sb("avx", [P, H, K, R])
        avxT = sb("avxT", [P, KT, L])
        xout = sb("xout", [P, H, D])

        ew_raw = Brep[:, 1, :]
        eb_raw = diagw[0:2].rearrange("p h e c -> p (h e c)")
        eb_hi = [dBu[0:2].rearrange("p s h l -> p (s h l)"), hst[0:2].rearrange("p s h l -> p (s h l)")]
        eb_rest = [eth[0:2].rearrange("p s c -> p (s c)"), avx[0:2].rearrange("p h k r -> p (h k r)")]
        convW = cst["conv_w"].rearrange("p (j e) -> p j e", j=DC)

        dA = [ps("dA0"), ps("dA1")]
        hT = ps("hT")
        hE = [ps("hE0"), ps("hE1")]
        pC = ps("pC")
        pT = ps("pT")
        pP = ps("pP")
        B_rows = nc.dram_tensor("B_rows", [B, DS * L], F32, kind="Internal").ap()

        early_in, late_in, ctx_in, x_in = sem("early_in"), sem("late_in"), sem("ctx_in"), sem("x_in")
        experts_in, expert_b_in = sem("experts_in"), sem("expert_b_in")
        zeroed, const_v, const_p, const_a = sem("zeroed"), sem("const_v"), sem("const_p"), sem("const_a")
        g_stats, g_mv, g_ve, g_rstd, zn_done, zT_done = (sig(n) for n in ("g_stats", "g_mv", "g_ve", "g_rstd", "zn_done", "zT_done"))
        zth_done, gate_done = sig("zth_done"), sig("gate_done")
        xc_done, uth_done, uhalf_done, u_done = sig("xc_done"), sig("uth_done"), sig("uhalf_done"), sig("u_done")
        dtB_mm, dtB_done, C_mm, C_done = sig("dtB_mm"), sig("dtB_done"), sig("C_mm"), sig("C_done")
        B_out, B_in = sig("B_out", 16), sig("B_in", 16)
        dt_mm, sp_abs_done, sp_exp_done, sp_log_done = sig("dt_mm"), sig("sp_abs_done"), sig("sp_exp_done"), sig("sp_log_done")
        sp_pos_done, delta_done, du_done = sig("sp_pos_done"), sig("delta_done"), sig("du_done")
        skip_mm, y_init = sig("skip_mm"), sig("y_init")
        q_mm, q_done, k_mm, k_done, en_mm = sig("q_mm"), sig("q_done"), sig("k_mm"), sig("k_done"), sig("en_mm")
        amax_done, aexp_done, arec_done, att_done, attT_mm, attT_done = (sig(n) for n in ("amax_done", "aexp_done", "arec_done", "att_done", "attT_mm", "attT_done"))
        dA_done, dBu_done, h_done, hT_done = sig("dA_done", DS), sig("dBu_done", DS), sig("h_done", DS), sig("hT_done", DS)
        y_done = sig("y_done", H * DS)
        gated_done, x1_done = sig("gated_done"), sig("x1_done")
        m_stats, m_mv, m_ve, m_rstd, xn1_done, xn1b_done, xn1T_mm, xh_done, xl_done = (
            sig(n) for n in ("m_stats", "m_mv", "m_ve", "m_rstd", "xn1_done", "xn1b_done", "xn1T_mm", "xh_done", "xl_done"))
        logit_mm, logit_done, top_done, topi_done, topf_done, gap_done, gexp_done, gden_done, w0_done, w1_done = (
            sig(n) for n in ("logit_mm", "logit_done", "top_done", "topi_done", "topf_done", "gap_done", "gexp_done", "gden_done", "w0_done", "w1_done"))
        pick_done, wfull_done, diagw_done = sig("pick_done"), sig("wfull_done"), sig("diagw_done", H)
        expert_mm, eth_done, eg_done, comb_mm = (sig(n, CHUNKS) for n in ("expert_mm", "eth_done", "eg_done", "comb_mm"))
        comb_done, proj_mm, yv_done, yss_done, yve_done, yrms_done, ynw_done, x2_done = (
            sig(n) for n in ("comb_done", "proj_mm", "yv_done", "yss_done", "yve_done", "yrms_done", "ynw_done", "x2_done"))
        t_stats, t_mv, t_ve, t_rstd = (sig(n, 2) for n in ("t_stats", "t_mv", "t_ve", "t_rstd"))
        xn2_done, xn2T_mm, xn2T_done, xm_mm, x3_done, xn3_done, xn3T_mm, xn3T_done = (
            sig(n) for n in ("xn2_done", "xn2T_mm", "xn2T_done", "xm_mm", "x3_done", "xn3_done", "xn3T_mm", "xn3T_done"))
        h1_mm, h1_done, lg2_mm, lg2_done, lmax_done, alpha_done, lrec_done = (
            sig(n) for n in ("h1_mm", "h1_done", "lg2_mm", "lg2_done", "lmax_done", "alpha_done", "lrec_done"))
        vx_mm, avx_done, avxT_mm, avxT_done = (sig(n, 2) for n in ("vx_mm", "avx_done", "avxT_mm", "avxT_done"))
        o_mm, xout_done, stored = sig("o_mm"), sig("xout_done"), sig("stored", 16)

        block = stack.enter_context(nc.Block())

        def run(slot, n_steps=B + 3):
            for t in range(n_steps):
                for s in range(SLOTS):
                    slot(t, s)

        @block.sync
        def _(sp):
            sp.dma_start(early_sb[:, :], early).then_inc(early_in, 16)
            sp.dma_start(ctx[:, :, DC - 1:], ctxT).then_inc(ctx_in, 16)
            sp.dma_start(dtp[:, :], dt_projT).then_inc(early_in, 16)
            sp.dma_start(xin[:, :, :, :], x).then_inc(x_in, 16)
            sp.dma_start(late_sb[:, :], late).then_inc(late_in, 16)
            sp.dma_start(ew_raw, experts).then_inc(experts_in, 16)
            sp.dma_start(eb_raw, expert_b).then_inc(expert_b_in, 16)
            sp.dma_start(sel_sb[:, :], rowsel).then_inc(expert_b_in, 16)

            def slot(t, s):
                if t < B and s == 10:
                    wait(sp, dtB_done, t)
                    sp.dma_start(B_rows[t].rearrange("(n l) -> n l", n=DS), dtB[DR:DR + DS, :]).then_inc(B_out.sem, 16)
                    wait(sp, B_out, t)
                    wait(sp, dBu_done, t - 2)
                    if t == 1:
                        sp.wait_ge(const_p, 1)
                    sp.dma_start(Brep[:, t % 2, :], B_rows[t:t + 1, :].to_broadcast([P, DS * L])).then_inc(B_in.sem, 16)
                b = t - 3
                if 0 <= b < B and s == SLOTS - 1:
                    wait(sp, xout_done, b)
                    sp.dma_start(out[:, b], xout[:, :, :]).then_inc(stored.sem, 16)

            run(slot)
            wait(sp, stored, B - 1)

        @block.gpsimd
        def _(pool):
            nc.gpsimd.memset(ctx[:, :, 0:DC - 1], 0.0)
            nc.gpsimd.memset(ones2[:, :], 1.0)
            nc.gpsimd.memset(neg_half[:, :], -0.5).then_inc(zeroed, 1)
            pool.wait_ge(const_a, 2)
            nc.gpsimd.tensor_tensor(ew_lo[:, :, :], ew_raw.rearrange("p (h c) -> p h c", h=H),
                                    ew_hi[:, :, :].bitcast(F32), ALU.subtract).then_inc(const_p, 1)

            def rsqrt(dst, src, ready, b, k, done):
                wait(pool, ready, b, k)
                nc.gpsimd.tensor_tensor(dst, src, neg_half[:, :], ALU.pow).then_inc(done.sem, 1)

            def slot(t, s):
                b = t
                if b < B:
                    if s == 2:
                        wait(pool, zn_done, b - 1)
                        rsqrt(grstd[:, :], gve[:, :], g_ve, b, None, g_rstd)
                    if s == 22:
                        wait(pool, delta_done, b)
                        wait(pool, u_done, b)
                        wait(pool, dBu_done, b - 2)
                        nc.gpsimd.tensor_tensor(du[:, b % 2], delta[:, b % 2], u[:, :, :], ALU.mult).then_inc(du_done.sem, 1)
                b = t - 1
                if 0 <= b < B and s % 2 == 0:
                    n = s // 2
                    if n == 0:
                        if b == 0:
                            pool.wait_ge(const_v, 5)
                        wait(pool, B_in, b)
                        wait(pool, du_done, b)
                    if n >= 2:
                        wait(pool, h_done, b, n - 1)
                    else:
                        wait(pool, h_done, b - 1, DS - 1 + n)
                    nc.gpsimd.tensor_tensor(
                        dBu[:, n % 2], du[:, b % 2],
                        Brep[:, b % 2, n * L:(n + 1) * L].unsqueeze(1).to_broadcast([P, H, L]), ALU.mult).then_inc(dBu_done.sem, 1)
                b = t - 2
                if 0 <= b < B:
                    if s == 1:
                        wait(pool, xn1_done, b - 1)
                        rsqrt(mrstd[:, :], mve[:, :], m_ve, b, None, m_rstd)
                    if s == 5:
                        if b == 0:
                            pool.wait_ge(late_in, 16)
                        wait(pool, xn1_done, b)
                        wait(pool, ynw_done, b - 2)
                        nc.gpsimd.tensor_tensor(xn1b[:, b % 2], xn1[:, :, :],
                                                cst["proj_b"].unsqueeze(1).to_broadcast([P, H, D]), ALU.add).then_inc(xn1b_done.sem, 1)
                    if s in (11, 13):
                        h = (s - 11) // 2
                        wait(pool, wfull_done, b)
                        wait(pool, comb_mm, b - 1)
                        nc.gpsimd.tensor_tensor(diagw[:, h], half_ident[:, :].unsqueeze(1).to_broadcast([P, E, P]),
                                                wfull[:, h, :].unsqueeze(2).to_broadcast([P, E, P]), ALU.mult).then_inc(diagw_done.sem, 1)
                b = t - 3
                if 0 <= b < B:
                    if s == 4:
                        wait(pool, ynw_done, b - 1)
                        rsqrt(yrms[:, :], yve[:, :], yve_done, b, None, yrms_done)
                    if s == 8:
                        wait(pool, xn2_done, b - 1)
                        rsqrt(trstd[:, 0, :], tve[:, 0, :], t_ve, b, 1, t_rstd)
                    if s == 14:
                        wait(pool, xn3_done, b - 1)
                        rsqrt(trstd[:, 1, :], tve[:, 1, :], t_ve, b, 2, t_rstd)

            pool.wait_ge(zeroed, 1)
            run(slot)

        @block.scalar
        def _(act):
            fn = nc.scalar.activation
            act.wait_ge(early_in, 32)
            fn(negA[:, :], cst["A_log"], ACT.Exp).then_inc(const_a, 1)
            act.wait_ge(experts_in, 16)
            fn(ew_hi[:, :, :], ew_raw.rearrange("p (h c) -> p h c", h=H), ACT.Copy).then_inc(const_a, 1)
            act.wait_ge(const_v, 1)

            def slot(t, s):
                b = t
                if b < B:
                    if s == 3:
                        wait(act, xc_done, b)
                        wait(act, gate_done, b - 1)
                        for h in range(H):
                            i = fn(uth[:, h], halves(pP[:, :])[:, h], ACT.Tanh, bias=half_cb[:, h:h + 1], scale=0.5)
                        i.then_inc(uth_done.sem, 1)
                    if s == 8:
                        wait(act, C_mm, b)
                        wait(act, B_out, b - 1)
                        wait(act, dt_mm, b - 1)
                        fn(dtB[:, :], pP[0:DR + DS, 0:L], ACT.Copy).then_inc(dtB_done.sem, 1)
                    if s == 9:
                        wait(act, C_mm, b)
                        wait(act, y_done, b - 2)
                        fn(Ct[:, b % 2], pP[:, L:L + H * DS].rearrange("p (h n) -> p h n", h=H), ACT.Copy).then_inc(C_done.sem, 1)
                    if s == 12:
                        wait(act, dt_mm, b)
                        wait(act, delta_done, b - 1)
                        for h in range(H):
                            i = fn(sp_abs[:, h], halves(pP[:, :])[:, h], ACT.Abs, bias=cst["dt_b"][:, h:h + 1])
                        i.then_inc(sp_abs_done.sem, 1)
                    if s == 13:
                        wait(act, sp_abs_done, b)
                        fn(sp_exp[:, :, :], sp_abs[:, :, :], ACT.Exp, scale=-1.0).then_inc(sp_exp_done.sem, 1)
                    if s == 14:
                        wait(act, sp_exp_done, b)
                        fn(sp_log[:, :, :], sp_exp[:, :, :], ACT.Ln, bias=1.0).then_inc(sp_log_done.sem, 1)
                    if s == 16:
                        wait(act, skip_mm, b)
                        wait(act, gated_done, b - 2)
                        fn(y[:, b % 2], halves(pP[:, :]), ACT.Copy).then_inc(y_init.sem, 1)
                    if s == 18:
                        wait(act, zT_done, b)
                        wait(act, u_done, b)
                        fn(zth[:, :, :], halves(pP[:, :]), ACT.Tanh, scale=0.5).then_inc(zth_done.sem, 1)
                    if s == 21:
                        wait(act, q_mm, b)
                        wait(act, en_mm, b - 1)
                        fn(qT[:, :], pP[:, 0:L], ACT.Identity, bias=cst["bq"]).then_inc(q_done.sem, 1)
                        fn(kT[:, :], pP[:, L:2 * L], ACT.Identity, bias=cst["bk"]).then_inc(k_done.sem, 1)
                    if s == 25:
                        wait(act, amax_done, b)
                        wait(act, attT_mm, b - 1)
                        for h in range(H):
                            i = fn(aexp[:, h], halves(pP[:, :])[:, h], ACT.Exp, bias=amax[:, h:h + 1], accum_out=asum[:, h:h + 1])
                        i.then_inc(aexp_done.sem, 1)
                    if s == 29:
                        wait(act, attT_mm, b)
                        wait(act, xm_mm, b - 3)
                        fn(attT[:, b % 3], halves(pP[:, :]), ACT.Copy).then_inc(attT_done.sem, 1)
                b = t - 1
                if 0 <= b < B and s % 2 == 0:
                    n = s // 2
                    if n == 0:
                        wait(act, delta_done, b)
                    if n >= 2:
                        wait(act, h_done, b, n - 1)
                    else:
                        wait(act, h_done, b - 1, DS - 1 + n)
                    for h in range(H):
                        i = fn(halves(dA[n % 2][:, :])[:, h, 1:], delta[:, b % 2, h, 1:], ACT.Exp,
                               scale=negA_n[:, h * DS + n:h * DS + n + 1])
                    i.then_inc(dA_done.sem, 1)
                b = t - 2
                if 0 <= b < B:
                    if s == 4:
                        wait(act, xn1T_mm, b)
                        wait(act, expert_mm, b - 1)
                        fn(xh[:, :, :], halves(hE[0][:, :]), ACT.Copy).then_inc(xh_done.sem, 1)
                    if s == 9:
                        wait(act, gap_done, b)
                        wait(act, w1_done, b - 1)
                        fn(gexp[:, :], gap[:, :], ACT.Exp).then_inc(gexp_done.sem, 1)
                    if s >= 10 and s % 2 == 0 and (s - 10) // 2 < CHUNKS:
                        c = (s - 10) // 2
                        wait(act, expert_mm, b, c + 1)
                        if c >= 2:
                            wait(act, comb_mm, b, c - 1)
                        else:
                            wait(act, comb_mm, b - 1, CHUNKS - 1 + c)
                        fn(eth[:, c % 2], hE[(c + 1) % 2][:, :], ACT.Tanh, scale=0.5).then_inc(eth_done.sem, 1)
                    if s == 28:
                        wait(act, comb_mm, b)
                        wait(act, proj_mm, b - 1)
                        fn(comb[:, :, :], halves(pC[:, :]), ACT.Copy).then_inc(comb_done.sem, 1)
                b = t - 3
                if 0 <= b < B:
                    if s == 2:
                        wait(act, yv_done, b)
                        wait(act, yve_done, b - 1)
                        wait(act, lg2_mm, b - 1)
                        for h in range(H):
                            i = fn(ysq[:, h], xn1b[:, b % 2, h], ACT.Square, accum_out=yss[:, h:h + 1])
                        i.then_inc(yss_done.sem, 1)
                    if s == 11:
                        wait(act, xn2T_mm, b)
                        wait(act, vx_mm, b - 1)
                        fn(xn2T[:, :, :], halves(pT[:, :]), ACT.Copy).then_inc(xn2T_done.sem, 1)
                    if s == 17:
                        wait(act, xn3T_mm, b)
                        wait(act, xm_mm, b)
                        fn(xn3T[:, :, :], halves(pT[:, :]), ACT.Copy).then_inc(xn3T_done.sem, 1)
                    if s == 19:
                        wait(act, h1_mm, b)
                        wait(act, x2_done, b)
                        wait(act, lg2_mm, b - 1)
                        for h in range(H):
                            i = fn(h1[:, h], halves(pT[:, :])[:, h], ACT.Relu, bias=cst["b1"][:, h:h + 1])
                        i.then_inc(h1_done.sem, 1)
                    if s == 22:
                        wait(act, lmax_done, b)
                        wait(act, avx_done, b - 1)
                        wait(act, lrec_done, b - 1)
                        for h in range(H):
                            i = fn(alpha[:, h], lg2[:, h], ACT.Exp, bias=lmax[:, h:h + 1], accum_out=lsum[:, h:h + 1])
                        i.then_inc(alpha_done.sem, 1)
                    if s in (27, 29):
                        k = (s - 27) // 2
                        wait(act, avxT_mm, b, k + 1)
                        wait(act, o_mm, b - 1)
                        fn(avxT[:, 2 * k:2 * k + 2], halves(pT[:, :]), ACT.Copy).then_inc(avxT_done.sem, 1)

            run(slot)

        @block.vector
        def _(dve):
            v = nc.vector
            for bank in dA:
                v.memset(halves(bank[:, :])[:, :, 0:1], 0.0)
            dve.wait_ge(early_in, 32)
            v.tensor_tensor(convW, convW, cst["in_projT"].unsqueeze(1).to_broadcast([P, DC, D]), ALU.mult)
            v.tensor_scalar(half_cb[:, :], cst["conv_b"], 0.5, None, ALU.mult)
            for h in range(H):
                v.tensor_scalar(diagD[:, h], ident, cst["Dskip"][:, h:h + 1], None, ALU.mult)
            v.tensor_scalar(half_ident[:, :], ident, 0.5, None, ALU.mult)
            dve.wait_ge(const_a, 1)
            v.tensor_scalar(negA_n[:, :], negA[:, :], -1.0, None, ALU.mult).then_inc(const_v, 1)

            def late_constants():
                dve.wait_ge(late_in, 16)
                dve.wait_ge(expert_b_in, 32)
                router = halves(cst["router"])
                v.tensor_copy(rw_hi[:, :, :], router)
                raw = eb_raw.rearrange("p (g c) -> p g c", g=2)
                for g in range(2):
                    v.tensor_copy(eb_hi[g].bitcast(F32R), raw[:, g])
                dve.wait_ge(zeroed, 1)
                v.tensor_copy(ones2r[:, :], ones2[:, :]).then_inc(const_v, 1)
                dve.wait_ge(const_v, 2)
                v.tensor_tensor(rw_lo[:, :, :], router, rw_hi[:, :, :].bitcast(F32), ALU.subtract)
                for g in range(2):
                    i = v.tensor_tensor(eb_rest[g], raw[:, g], eb_hi[g], ALU.subtract)
                i.then_inc(const_v, 1)
                dve.wait_ge(const_v, 3)
                for g in range(2):
                    i = v.tensor_scalar(raw[:, g], eb_rest[g], sel_sb[:, 1:2], None, ALU.mult)
                i.then_inc(const_v, 1)
                dve.wait_ge(const_v, 4)
                for g in range(2):
                    i = v.scalar_tensor_tensor(eb_rows[:, g * E * D // 2:(g + 1) * E * D // 2], eb_hi[g], sel_sb[:, 0:1], raw[:, g],
                                               ALU.mult, ALU.add)
                i.then_inc(const_v, 1)

            def stats(src, st, mv, ve, eps, s_stats, s_mv, s_ve, b, k):
                for h in range(H):
                    i = v.bn_stats(st[:, h], src[:, h])
                i.then_inc(s_stats.sem, 1)
                wait(dve, s_stats, b, k)
                for h in range(H):
                    i = v.bn_aggr(mv[:, h], st[:, h])
                i.then_inc(s_mv.sem, 1)
                wait(dve, s_mv, b, k)
                v.tensor_scalar(ve, mv[:, :, 1], eps, None, ALU.add).then_inc(s_ve.sem, 1)

            def normalize(dst, src, mv, rstd, s_rstd, b, k, done):
                wait(dve, s_rstd, b, k)
                for h in range(H):
                    i = v.tensor_scalar(dst[:, h], src[:, h], mv[:, h, 0:1], rstd[:, h:h + 1], ALU.subtract, ALU.mult)
                i.then_inc(done.sem, 1)

            def slot(t, s):
                b = t
                if b < B:
                    if s == 0:
                        if b == 0:
                            dve.wait_ge(x_in, 16)
                        stats(xin[:, b], gst, gmv, gve[:, :], 1e-5, g_stats, g_mv, g_ve, b, None)
                    if s == 4:
                        wait(dve, uth_done, b)
                        wait(dve, delta_done, b - 1)
                        for h in range(H):
                            i = v.tensor_scalar(uhalf[:, h], halves(pP[:, :])[:, h], cst["conv_b"][:, h:h + 1], 0.5, ALU.add, ALU.mult)
                        i.then_inc(uhalf_done.sem, 1)
                    if s == 5:
                        wait(dve, uhalf_done, b)
                        wait(dve, du_done, b - 1)
                        wait(dve, skip_mm, b - 1)
                        v.scalar_tensor_tensor(u[:, :, :], uth[:, :, :], 1.0, uhalf[:, :, :], ALU.add, ALU.mult).then_inc(u_done.sem, 1)
                    if s == 6:
                        wait(dve, zT_done, b - 1)
                        normalize(zn, xin[:, b], gmv, grstd, g_rstd, b, None, zn_done)
                    if s == 13:
                        wait(dve, sp_abs_done, b)
                        for h in range(H):
                            i = v.tensor_scalar(sp_pos[:, h], halves(pP[:, :])[:, h], cst["dt_b"][:, h:h + 1], 0.0, ALU.add, ALU.max)
                        i.then_inc(sp_pos_done.sem, 1)
                    if s == 17:
                        wait(dve, sp_pos_done, b)
                        wait(dve, sp_log_done, b)
                        wait(dve, dA_done, b - 2)
                        v.tensor_tensor(delta[:, b % 2], sp_pos[:, :, :], sp_log[:, :, :], ALU.add).then_inc(delta_done.sem, 1)
                    if s == 19:
                        wait(dve, zth_done, b)
                        wait(dve, gated_done, b - 2)
                        v.scalar_tensor_tensor(gate[:, b % 2], zth[:, :, :], 1.0, halves(pP[:, :]), ALU.add, ALU.mult).then_inc(gate_done.sem, 1)
                    if s == 24:
                        wait(dve, en_mm, b)
                        wait(dve, aexp_done, b - 1)
                        v.tensor_reduce(amax[:, :], halves(pP[:, :]), AX.X, ALU.max, negate=True).then_inc(amax_done.sem, 1)
                    if s == 26:
                        wait(dve, aexp_done, b)
                        v.reciprocal(arec[:, :], asum[:, :]).then_inc(arec_done.sem, 1)
                        wait(dve, arec_done, b)
                        for h in range(H):
                            i = v.tensor_scalar(att[:, h], aexp[:, h], arec[:, h:h + 1], None, ALU.mult)
                        i.then_inc(att_done.sem, 1)
                b = t - 1
                if 0 <= b < B and s % 2 == 0:
                    n = s // 2
                    wait(dve, dA_done, b, n + 1)
                    wait(dve, dBu_done, b, n + 1)
                    if n >= 2:
                        wait(dve, hT_done, b, n - 1)
                    else:
                        wait(dve, hT_done, b - 1, DS - 1 + n)
                    v.tensor_tensor_scan(out=hst[:, n % 2].rearrange("p h l -> p (h l)"), data0=dA[n % 2][:, :],
                                         data1=dBu[:, n % 2].rearrange("p h l -> p (h l)"), initial=0.0,
                                         op0=ALU.mult, op1=ALU.add).then_inc(h_done.sem, 1)
                if 0 <= b < B and s % 2 == 1:
                    for n in ([s // 2 - 1] if s < SLOTS - 1 else [DS - 2, DS - 1]):
                        if n < 0:
                            continue
                        if n == 0:
                            wait(dve, y_init, b)
                            wait(dve, C_done, b)
                        wait(dve, hT_done, b, n + 1)
                        for h in range(H):
                            if n:
                                wait(dve, y_done, b, H * (n - 1) + h + 1)
                            v.scalar_tensor_tensor(y[:, b % 2, h], halves(hT[:, :])[:, h], Ct[:, b % 2, h, n:n + 1],
                                                   y[:, b % 2, h], ALU.mult, ALU.add).then_inc(y_done.sem, 1)
                    if s == SLOTS - 1:
                        wait(dve, y_done, b)
                        wait(dve, gate_done, b)
                        wait(dve, x1_done, b - 1)
                        v.scalar_tensor_tensor(y[:, b % 2], y[:, b % 2], 0.5, gate[:, b % 2], ALU.mult, ALU.mult).then_inc(gated_done.sem, 1)
                        wait(dve, gated_done, b)
                        wait(dve, x2_done, b - 2)
                        v.tensor_tensor(x1[:, b % 2], y[:, b % 2], xin[:, b], ALU.add).then_inc(x1_done.sem, 1)
                b = t - 2
                if 0 <= b < B:
                    if s == 0:
                        wait(dve, x1_done, b)
                        stats(x1[:, b % 2], mst, mmv, mve[:, :], 1e-5, m_stats, m_mv, m_ve, b, None)
                    if s == 2:
                        wait(dve, xn1b_done, b - 1)
                        wait(dve, xn1T_mm, b - 1)
                        normalize(xn1, x1[:, b % 2], mmv, mrstd, m_rstd, b, None, xn1_done)
                    if s == 5:
                        wait(dve, xh_done, b)
                        wait(dve, expert_mm, b - 1)
                        v.tensor_tensor(xl[:, :, :], halves(hE[0][:, :]), xh[:, :, :].bitcast(F32), ALU.subtract).then_inc(xl_done.sem, 1)
                    if s == 8:
                        wait(dve, logit_mm, b)
                        v.tensor_tensor(logit[:, :, :], pC[:, 0:H * E].rearrange("p (h e) -> p h e", h=H),
                                        cst["router_b"].unsqueeze(1).to_broadcast([P, H, E]), ALU.add).then_inc(logit_done.sem, 1)
                        wait(dve, logit_done, b)
                        for h in range(H):
                            i = v.max(top[:, h], logit[:, h])
                        i.then_inc(top_done.sem, 1)
                        wait(dve, top_done, b)
                        v.tensor_tensor(gap[:, :], top[:, :, 1], top[:, :, 0], ALU.subtract).then_inc(gap_done.sem, 1)
                        for h in range(H):
                            i = v.max_index(topi[:, h], top[:, h], logit[:, h])
                        i.then_inc(topi_done.sem, 1)
                        wait(dve, topi_done, b)
                        v.tensor_copy(topf[:, :, :], topi[:, :, :]).then_inc(topf_done.sem, 1)
                    if s == 10:
                        wait(dve, gexp_done, b)
                        v.tensor_scalar(gden[:, :], gexp[:, :], 1.0, None, ALU.add).then_inc(gden_done.sem, 1)
                        wait(dve, gden_done, b)
                        v.reciprocal(w0[:, :], gden[:, :]).then_inc(w0_done.sem, 1)
                        wait(dve, w0_done, b)
                        v.tensor_tensor(w1[:, :], gexp[:, :], w0[:, :], ALU.mult).then_inc(w1_done.sem, 1)
                        wait(dve, w1_done, b)
                        wait(dve, topf_done, b)
                        for h in range(H):
                            v.tensor_scalar(pick0[:, h], cst["iota"], topf[:, h, 0:1], w0[:, h:h + 1], ALU.is_equal, ALU.mult)
                            i = v.tensor_scalar(pick1[:, h], cst["iota"], topf[:, h, 1:2], w1[:, h:h + 1], ALU.is_equal, ALU.mult)
                        i.then_inc(pick_done.sem, 1)
                        wait(dve, pick_done, b)
                        wait(dve, diagw_done, b - 1)
                        v.tensor_tensor(wfull[:, :, :], pick0[:, :, :], pick1[:, :, :], ALU.add).then_inc(wfull_done.sem, 1)
                    if s >= 11 and s % 2 == 1 and (s - 11) // 2 < CHUNKS:
                        c = (s - 11) // 2
                        wait(dve, eth_done, b, c + 1)
                        v.scalar_tensor_tensor(eg[:, c % 2], eth[:, c % 2], 1.0, hE[(c + 1) % 2][:, :], ALU.add, ALU.mult).then_inc(eg_done.sem, 1)
                b = t - 3
                if 0 <= b < B:
                    if s == 1:
                        wait(dve, proj_mm, b)
                        wait(dve, xn1b_done, b)
                        wait(dve, ynw_done, b - 1)
                        v.tensor_tensor(xn1b[:, b % 2], halves(pT[:, :]), xn1b[:, b % 2], ALU.add).then_inc(yv_done.sem, 1)
                    if s == 3:
                        wait(dve, yss_done, b)
                        wait(dve, yrms_done, b - 1)
                        v.tensor_scalar(yve[:, :], yss[:, :], 1.0 / D, 1e-6, ALU.mult, ALU.add).then_inc(yve_done.sem, 1)
                    if s == 6:
                        wait(dve, yrms_done, b)
                        for h in range(H):
                            i = v.scalar_tensor_tensor(ynw[:, h], xn1b[:, b % 2, h], yrms[:, h:h + 1], cst["norm_w"], ALU.mult, ALU.mult)
                        i.then_inc(ynw_done.sem, 1)
                        wait(dve, ynw_done, b)
                        wait(dve, x3_done, b - 1)
                        v.tensor_tensor(x2[:, :, :], ynw[:, :, :], x1[:, b % 2], ALU.add).then_inc(x2_done.sem, 1)
                        wait(dve, x2_done, b)
                        stats(x2, tst[:, 0], tmv[:, 0], tve[:, 0, :], 1e-5, t_stats, t_mv, t_ve, b, 1)
                    if s == 9:
                        wait(dve, xn3T_mm, b - 1)
                        normalize(xn2, x2, tmv[:, 0], trstd[:, 0], t_rstd, b, 1, xn2_done)
                    if s == 13:
                        wait(dve, xm_mm, b)
                        wait(dve, xout_done, b - 1)
                        v.tensor_tensor(x3[:, :, :], halves(pT[:, :]), x2[:, :, :], ALU.add).then_inc(x3_done.sem, 1)
                        wait(dve, x3_done, b)
                        stats(x3, tst[:, 1], tmv[:, 1], tve[:, 1, :], 1e-5, t_stats, t_mv, t_ve, b, 2)
                    if s == 15:
                        wait(dve, xn2T_mm, b)
                        normalize(xn3, x3, tmv[:, 1], trstd[:, 1], t_rstd, b, 2, xn3_done)
                    if s == 21:
                        wait(dve, lg2_mm, b)
                        wait(dve, alpha_done, b - 1)
                        v.tensor_tensor(lg2[:, :, :], pT[:, 0:H * K].rearrange("p (h k) -> p h k", h=H),
                                        cst["b2"].unsqueeze(1).to_broadcast([P, H, K]), ALU.add).then_inc(lg2_done.sem, 1)
                        wait(dve, lg2_done, b)
                        v.tensor_reduce(lmax[:, :], lg2[:, :, :], AX.X, ALU.max, negate=True).then_inc(lmax_done.sem, 1)
                    if s in (23, 25):
                        h = (s - 23) // 2
                        wait(dve, vx_mm, b, h + 1)
                        wait(dve, alpha_done, b)
                        wait(dve, avxT_mm, b - 1)
                        v.tensor_tensor(avx[:, h], pT[:, :].rearrange("p (k r) -> p k r", k=K),
                                        alpha[:, h].unsqueeze(2).to_broadcast([P, K, R]), ALU.mult).then_inc(avx_done.sem, 1)
                    if s == 26:
                        wait(dve, xout_done, b - 1)
                        v.reciprocal(lrec[:, :], lsum[:, :]).then_inc(lrec_done.sem, 1)
                    if s == 31:
                        wait(dve, o_mm, b)
                        wait(dve, lrec_done, b)
                        wait(dve, stored, b - 1)
                        for h in range(H):
                            i = v.scalar_tensor_tensor(xout[:, h], halves(pT[:, :])[:, h], lrec[:, h:h + 1],
                                                       x3[:, h], ALU.mult, ALU.add)
                        i.then_inc(xout_done.sem, 1)
                if t == 0 and s == SLOTS - 1:
                    late_constants()

            run(slot)

        @block.tensor
        def _(pe):
            def mm(out_, lhsT, rhs, first, last, **kw):
                return nc.tensor.matmul(out_, lhsT, rhs, start=first, stop=last, **kw)

            def transposes(dst, src):
                for j in range(H):
                    for i in range(H):
                        last = nc.tensor.transpose(halves(dst)[:, j, i * P:(i + 1) * P], src[:, i, j * P:(j + 1) * P], ident)
                return last

            def slot(t, s):
                b = t
                if b < B:
                    if s == 2:
                        if b == 0:
                            pe.wait_ge(ctx_in, 16)
                            pe.wait_ge(zeroed, 1)
                            pe.wait_ge(const_v, 1)
                        wait(pe, attT_done, b - 1)
                        for h in range(H):
                            for j in range(DC):
                                i = mm(halves(pP[:, :])[:, h], convW[:, j, h * P:(h + 1) * P], ctx[:, b, j:j + L], j == 0, j == DC - 1)
                        i.then_inc(xc_done.sem, 1)
                    if s == 7:
                        wait(pe, u_done, b)
                        for h in range(H):
                            i = mm(pP[0:DR + DS, 0:L], xproj[:, h, 0:DR + DS], u[:, h], h == 0, h == H - 1)
                        i.then_inc(dtB_mm.sem, 1)
                        for g in range(H):
                            for h in range(H):
                                i = mm(pP[:, L + g * DS:L + (g + 1) * DS], u[:, h, g * P:(g + 1) * P], xproj[:, h, DR + DS:], h == 0, h == H - 1)
                        i.then_inc(C_mm.sem, 1)
                    if s == 11:
                        wait(pe, dtB_done, b)
                        wait(pe, C_done, b)
                        for h in range(H):
                            i = mm(halves(pP[:, :])[:, h], dtp[:, h * P:(h + 1) * P], dtB[0:DR, :], True, True)
                        i.then_inc(dt_mm.sem, 1)
                    if s == 15:
                        wait(pe, sp_abs_done, b)
                        wait(pe, sp_pos_done, b)
                        for g in range(H):
                            for h in range(H):
                                i = mm(halves(pP[:, :])[:, g, h * P:(h + 1) * P], u[:, h, g * P:(g + 1) * P], diagD[:, h], True, True)
                        i.then_inc(skip_mm.sem, 1)
                    if s == 17:
                        wait(pe, y_init, b)
                        wait(pe, zn_done, b)
                        transposes(pP[:, :], zn).then_inc(zT_done.sem, 1)
                    if s == 20:
                        if b == 0:
                            pe.wait_ge(late_in, 16)
                        wait(pe, gate_done, b)
                        mm(pP[:, 0:L], cst["WqT"], ctx[:, b, DC - 1:], True, True)
                        mm(pP[:, L:2 * L], cst["WkT"], ctx[:, b, DC - 1:], True, True).then_inc(q_mm.sem, 1)
                    if s == 23:
                        wait(pe, q_done, b)
                        wait(pe, k_done, b)
                        for h in range(H):
                            i = mm(halves(pP[:, :])[:, h], qT[:, h * P:(h + 1) * P], kT[:, :], True, True)
                        i.then_inc(en_mm.sem, 1)
                    if s == 28:
                        wait(pe, att_done, b)
                        transposes(pP[:, :], att).then_inc(attT_mm.sem, 1)
                b = t - 1
                if 0 <= b < B and s % 2 == 1:
                    for n in ([s // 2] if s < SLOTS - 1 else [DS - 1]):
                        wait(pe, h_done, b, n + 1)
                        wait(pe, y_done, b if n else b - 1, H * n if n else None)
                        transposes(hT[:, :], hst[:, n % 2]).then_inc(hT_done.sem, 1)
                b = t - 2
                if 0 <= b < B:
                    if s == 3:
                        wait(pe, xn1_done, b)
                        wait(pe, eg_done, b - 1)
                        transposes(hE[0][:, :], xn1).then_inc(xn1T_mm.sem, 1)
                    if s == 6:
                        if b == 0:
                            pe.wait_ge(const_v, 5)
                            pe.wait_ge(const_p, 1)
                        wait(pe, xh_done, b)
                        wait(pe, xl_done, b)
                        wait(pe, comb_done, b - 1)
                        for g in range(H):
                            n = 0
                            for h in range(H):
                                for a, w in ((xh, rw_hi), (xl, rw_hi), (xh, rw_lo)):
                                    i = mm(pC[:, g * E:(g + 1) * E], a[:, h, g * P:(g + 1) * P], w[:, h], n == 0, n == 3 * H - 1)
                                    n += 1
                        i.then_inc(logit_mm.sem, 1)
                    if s >= 8 and s % 2 == 0 and (s - 8) // 2 < CHUNKS:
                        c = (s - 8) // 2
                        g, e = c // (E // 2), c % (E // 2)
                        if c >= 2:
                            wait(pe, eg_done, b, c - 1)
                        cols = slice(e * 2 * D, (e + 1) * 2 * D)
                        bank = hE[(c + 1) % 2]
                        for h in range(H):
                            for n, (a, w) in enumerate(((xh, ew_hi), (xl, ew_hi), (xh, ew_lo))):
                                mm(bank[:, :], a[:, h, g * P:(g + 1) * P], w[:, h, cols], h == 0 and n == 0, False)
                        mm(bank[:, :], ones2r[:, :], eb_rows[:, cols], False, True).then_inc(expert_mm.sem, 1)
                    if s >= 12 and s % 2 == 0 and (s - 12) // 2 < CHUNKS:
                        c = (s - 12) // 2
                        g, e = c // (E // 2), c % (E // 2)
                        wait(pe, eg_done, b, c + 1)
                        wait(pe, diagw_done, b, g + 1)
                        for k in range(2):
                            for h in range(H):
                                i = mm(halves(pC[:, :])[:, h, g * P:(g + 1) * P], eg[:, c % 2, k * D + h * P:k * D + (h + 1) * P],
                                       diagw[:, g, 2 * e + k], c == 0 and k == 0 and h == 0,
                                       c == CHUNKS - 1 and k == 1 and h == H - 1, skip_group_check=True)
                        i.then_inc(comb_mm.sem, 1)
                b = t - 3
                if 0 <= b < B:
                    if s == 0:
                        wait(pe, comb_done, b)
                        wait(pe, xout_done, b - 1)
                        for g in range(H):
                            for h in range(H):
                                i = mm(halves(pT[:, :])[:, g], comb[:, h, g * P:(g + 1) * P], halves(cst["proj"])[:, h], h == 0, h == H - 1)
                        i.then_inc(proj_mm.sem, 1)
                    if s == 10:
                        wait(pe, xn2_done, b)
                        wait(pe, yv_done, b)
                        transposes(pT[:, :], xn2).then_inc(xn2T_mm.sem, 1)
                    if s == 12:
                        wait(pe, xn2T_done, b)
                        wait(pe, attT_done, b)
                        for g in range(H):
                            for h in range(H):
                                i = mm(halves(pT[:, :])[:, g], xn2T[:, h, g * P:(g + 1) * P], attT[:, b % 3, h], h == 0, h == H - 1)
                        i.then_inc(xm_mm.sem, 1)
                    if s == 16:
                        wait(pe, xn3_done, b)
                        wait(pe, x3_done, b)
                        transposes(pT[:, :], xn3).then_inc(xn3T_mm.sem, 1)
                    if s == 18:
                        wait(pe, xn3T_done, b)
                        w1v = halves(cst["W1"])
                        for g in range(H):
                            for h in range(H):
                                i = mm(halves(pT[:, :])[:, g], w1v[:, h, g * P:(g + 1) * P], xn3T[:, h], h == 0, h == H - 1)
                        i.then_inc(h1_mm.sem, 1)
                    if s == 20:
                        wait(pe, h1_done, b)
                        for g in range(H):
                            for h in range(H):
                                i = mm(pT[:, g * K:(g + 1) * K], h1[:, h, g * P:(g + 1) * P], halves(cst["W2"])[:, h], h == 0, h == H - 1)
                        i.then_inc(lg2_mm.sem, 1)
                    if s in (22, 24):
                        g = (s - 22) // 2
                        if g == 0:
                            wait(pe, lg2_done, b)
                        else:
                            wait(pe, avx_done, b, 1)
                        for h in range(H):
                            i = mm(pT[:, :], xn3T[:, h, g * P:(g + 1) * P], halves(cst["VT"])[:, h], h == 0, h == H - 1)
                        i.then_inc(vx_mm.sem, 1)
                    if s in (26, 28):
                        k = (s - 26) // 2
                        wait(pe, avx_done, b)
                        if k:
                            wait(pe, avxT_done, b, 1)
                        for j in range(2):
                            for g in range(H):
                                src = avx[:, g].rearrange("p k r -> p (k r)")
                                i = nc.tensor.transpose(halves(pT[:, :])[:, j, g * P:(g + 1) * P], src[:, (2 * k + j) * P:(2 * k + j + 1) * P], ident)
                        i.then_inc(avxT_mm.sem, 1)
                    if s == 30:
                        wait(pe, avxT_done, b)
                        ut = cst["UT"].rearrange("p (k d) -> p k d", k=KT)
                        for g in range(H):
                            for k in range(KT):
                                i = mm(halves(pT[:, :])[:, g], avxT[:, k, g * P:(g + 1) * P], ut[:, k], k == 0, k == KT - 1)
                        i.then_inc(o_mm.sem, 1)

            run(slot)


def kernel(**inputs):
    import numpy as np
    import concourse.bacc as bacc
    from concourse.bass_utils import run_bass_kernel_spmd

    a = {k: np.asarray(v) for k, v in inputs.items()}

    def halves(m):
        return m.reshape(-1, P, m.shape[1]).transpose(1, 0, 2).reshape(P, -1)

    def everywhere(row):
        return np.broadcast_to(row.reshape(1, -1), (P, row.size))

    laid = {
        "in_projT": a["L0_xattn_in_proj_w"].T, "conv_w": everywhere(a["L0_xattn_conv_w"].T),
        "conv_b": halves(a["L0_xattn_conv_b"][:, None]), "x_projT": halves(a["L0_xattn_x_proj_w"].T),
        "dt_b": halves(a["L0_xattn_dt_proj_b"][:, None]), "Dskip": halves(a["L0_xattn_D"][:, None]),
        "A_log": halves(a["L0_xattn_A_log"]), "ident": np.eye(P, dtype=np.float32),
        "WqT": a["L1_xattn_Wq"].T, "WkT": a["L1_xattn_Wk"].T, "bq": a["L1_xattn_bq"][:, None], "bk": a["L1_xattn_bk"][:, None],
        "router": halves(a["L0_ffn_router_w"]), "router_b": everywhere(a["L0_ffn_router_b"]),
        "proj": halves(a["L0_ffn_proj_w"]), "proj_b": everywhere(a["L0_ffn_proj_b"]), "norm_w": everywhere(a["L0_ffn_norm_w"]),
        "W1": halves(a["L1_ffn_W1"]), "b1": halves(a["L1_ffn_b1"][:, None]), "W2": halves(a["L1_ffn_W2"]),
        "b2": everywhere(a["L1_ffn_b2"]), "VT": halves(a["L1_ffn_V"].reshape(K * R, D).T),
        "UT": halves(a["L1_ffn_U"].transpose(0, 2, 1).reshape(K * R, D)), "iota": everywhere(np.arange(E, dtype=np.float32)),
    }
    arrays = {
        "early": np.concatenate([laid[n] for n, _ in EARLY], axis=1),
        "late": np.concatenate([laid[n] for n, _ in LATE], axis=1),
        "experts": halves(a["L0_ffn_expert_w"].transpose(1, 0, 2).reshape(D, E * D)),
        "expert_b": np.broadcast_to(a["L0_ffn_expert_b"].reshape(1, -1), (2, E * D)),
        "rowsel": np.eye(2, dtype=np.float32),
        "dt_projT": a["L0_xattn_dt_proj_w"].T,
        "ctxT": a["ctx_1024"].transpose(2, 0, 1),
        "x": a["x"].reshape(B, H, P, D).transpose(2, 0, 1, 3),
    }
    arrays = {k: np.ascontiguousarray(m) for k, m in arrays.items()}
    nc = bacc.Bacc("TRN2", target_bir_lowering=False, num_devices=1)
    args = [nc.dram_tensor(k, m.shape, mybir.dt.from_np(m.dtype), kind="ExternalInput").ap() for k, m in arrays.items()]
    out = nc.dram_tensor("out", (P, B, H, D), F32, kind="ExternalOutput").ap()
    build(nc, *args, out)
    got = run_bass_kernel_spmd(nc, [arrays], core_ids=[0]).results[0]["out"]
    return np.ascontiguousarray(got.transpose(1, 2, 0, 3)).reshape(B, L, D)
```

```python
import concourse.bass as bass
from concourse import mybir
from contextlib import ExitStack

F32 = mybir.dt.float32
F32R = mybir.dt.float32r
U32 = mybir.dt.uint32
ALU = mybir.AluOpType
ACT = mybir.ActivationFunctionType
AX = mybir.AxisListType

P = 128
B, L, D, C = 4, 256, 256, 128
H = D // P
DS, DC, DR = 16, 4, 8
E = 8
K, R = 8, 64
KT = K * R // P
CHUNKS = E // 2
UNITS = B * H
SLOTS = 4 * DS
HALF = SLOTS // H
PIECES = 8

EARLY = [("in_projT", D), ("conv_w", DC * D), ("conv_b", H), ("x_projT", H * (DR + 2 * DS)), ("dt_b", H),
         ("Dskip", H), ("A_log", H * DS), ("ident", P)]
LATE = [("WqT", P), ("WkT", P), ("bq", 1), ("bk", 1), ("router", H * E), ("router_b", E), ("proj", H * D),
        ("proj_b", D), ("norm_w", D), ("W1", H * D), ("b1", H), ("W2", H * K), ("b2", K), ("VT", H * K * R),
        ("UT", KT * D), ("iota", E)]


WHEN = {
    "sp": {
        "B_rows": 73, "eb_rows": 166, "store": 370,
    },
    "pool": {
        "g_rstd": 22, "du": 56, "dBu": (60, 62, 68, 71, 79, 79, 85, 88, 91, 94, 97, 102, 111, 113, 118, 121),
        "m_rstd": 9, "xn1b": 18, "esum": (35, 40, 41), "comb": 42, "yrms": 58, "a_rstd": 65, "b_rstd": 78,
    },
    "act": {
        "uth": 7, "dtB": 15, "C": 15, "sp_abs": 17, "sp_exp": 18, "sp_log": 25, "y_init": 31, "zth": 39,
        "experts_hi": 16, "dA": (50, 62, 69, 69, 74, 78, 80, 83, 88, 92, 100, 103, 105, 110, 111, 112), "q": 112,
        "aexp": 122, "attT": 131, "xh": 10, "gexp": 17, "silu": (24, 27, 30, 33), "combT": 41, "yss": 48, "xn2T": 66,
        "xn3T": 78, "h1": 86, "alpha": 88, "avxT": 98,
    },
    "dve": {
        "g_stats": 9, "uhalf": 18, "u": 18, "zn": 29, "sp_pos": 28, "delta": 34, "gate": 47, "split_small": 79,
        "split_experts": (21, 22, 29, 62),
        "scan": (65, 70, 79, 82, 87, 89, 90, 94, 98, 102, 109, 111, 115, 119, 121, 124),
        "y": (72, 79, 85, 87, 89, 92, 97, 100, 105, 110, 112, 118, 119, 122, 127, 133), "x1": 135, "amax": 122,
        "arec": 131, "m_stats": 8, "xn1": 11, "xl": 21, "logit": 23, "gden": 26, "eg": (31, 35, 38, 42), "yv": 54,
        "yve": 57, "ynw": 63, "xn2": 69, "x3": 74, "xn3": 81, "lg2": 91, "avx": 99, "xout": 111,
    },
    "pe": {
        "xc": 3, "dtB": 17, "dt": 20, "skip": 28, "zT": 33,
        "hT": (63, 68, 74, 82, 86, 88, 91, 93, 95, 99, 100, 106, 113, 118, 120, 124), "q": 101, "en": 115,
        "attT": 125, "xn1T": 5, "logit": 18, "expert": (23, 24, 28, 29), "combT": 36, "proj": 48, "xn2T": 62,
        "xm": 64, "xn3T": 76, "h1": 86, "lg2": 87, "vx": 89, "avxT": 94, "o": 99,
    },
}

BATCH_AT = (0, 64, 128, 192)
UNIT_AT = (128, 160, 192, 224, 256, 288, 320, 352)


class Signal:

    def __init__(self, handle, per=1):
        self.sem, self.per = handle, per

    def value(self, b, k=None):
        return self.per * b + (self.per if k is None else k)


def wait(engine, signal, b, k=None):
    if b >= 0:
        engine.wait_ge(signal.sem, signal.value(b, k))


def build(nc, early, late, experts, expert_b, dt_projT, ctxT, x, out):
    with ExitStack() as stack:
        def sb(name, shape, dt=F32):
            return stack.enter_context(nc.sbuf_tensor(name, shape, dt))

        def ps(name):
            return stack.enter_context(nc.psum_tensor(name, [P, 512], F32))

        def sem(name):
            return stack.enter_context(nc.semaphore(name))

        def sig(name, per=1):
            return Signal(sem(name), per)

        def halves(t):
            return t.rearrange("p (h c) -> p h c", h=H)

        early_sb = sb("early_sb", [P, sum(n for _, n in EARLY)])
        late_sb = sb("late_sb", [P, sum(n for _, n in LATE)])
        cst = {}
        for tile, table in ((early_sb, EARLY), (late_sb, LATE)):
            at = 0
            for name, n in table:
                cst[name] = tile[:, at:at + n]
                at += n
        ident = cst["ident"]
        xproj = halves(cst["x_projT"])
        dtp = sb("dtp", [DR, D])
        ew_hi = sb("ew_hi", [P, H, E * D], F32R)
        ew_lo = sb("ew_lo", [P, H, E * D], F32R)
        ew_hi_f = ew_hi[:, :, :].rearrange("p h c -> p (h c)").bitcast(F32)
        ew_lo_f = ew_lo[:, :, :].rearrange("p h c -> p (h c)")
        rw_hi = sb("rw_hi", [P, H, E], F32R)
        rw_lo = sb("rw_lo", [P, H, E], F32R)
        eb_raw = sb("eb_raw", [P, E * D // P])
        eb_hi = sb("eb_hi", [P, E * D // P], F32R)
        eb_lo = sb("eb_lo", [P, E * D // P], F32R)
        eb_rows = sb("eb_rows", [2, E * D], F32R)
        ones2 = sb("ones2", [2, P])
        ones2r = sb("ones2r", [2, P], F32R)
        negA = sb("negA", [P, H * DS])
        negA_n = sb("negA_n", [P, H * DS])
        half_cb = sb("half_cb", [P, H])
        diagD = sb("diagD", [P, H, P])
        neg_half = sb("neg_half", [P, H])
        ctx = sb("ctx", [P, B, DC - 1 + L])
        xin = sb("xin", [P, B, H, D])
        gst = sb("gst", [P, H, 6])
        gmv = sb("gmv", [P, H, 2])
        gve = sb("gve", [P, H])
        grstd = sb("grstd", [P, H])
        zn = sb("zn", [P, H, L])
        gate = sb("gate", [P, 2, H, D])
        uth = sb("uth", [P, H, L])
        zth = uth
        uhalf = sb("uhalf", [P, H, L])
        u = sb("u", [P, H, L])
        dtB = sb("dtB", [DR + DS, L])
        Ct = sb("Ct", [P, 2, H, DS])
        sp_abs = sb("sp_abs", [P, H, L])
        sp_exp = sp_log = sp_abs
        sp_pos = uhalf
        delta = sb("delta", [P, 2, H, L])
        du = sb("du", [P, 2, H, L])
        Brep = sb("Brep", [P, 2, DS * L])
        y = sb("y", [P, 2, H, D])
        qT = sb("qT", [P, L])
        kT = sb("kT", [P, L])
        amax = sb("amax", [P, H])
        aexp = sb("aexp", [P, H, L])
        asum = sb("asum", [P, H])
        arec = sb("arec", [P, H])
        att = aexp
        attT = sb("attT", [P, 3, H, L])
        dBu = sb("dBu", [P, 2, H, L])
        hst = sb("hst", [P, 2, H, L])
        x1 = sb("x1", [P, 2, H, D])
        mst = sb("mst", [P, 6])
        mmv = sb("mmv", [P, 2])
        mve = sb("mve", [P, 1])
        mrstd = sb("mrstd", [P, 1])
        xn1 = sb("xn1", [P, D])
        xn1b = sb("xn1b", [P, 2, D])
        xh = sb("xh", [P, H, P], F32R)
        xl = sb("xl", [P, H, P], F32R)
        logit = sb("logit", [P, E])
        top = sb("top", [P, 8])
        topi = sb("topi", [P, 8], U32)
        topf = sb("topf", [P, 8])
        gap = sb("gap", [P, 1])
        gexp = sb("gexp", [P, 1])
        gden = sb("gden", [P, 1])
        w0 = sb("w0", [P, 1])
        w1 = sb("w1", [P, 1])
        pick0 = sb("pick0", [P, E])
        pick1 = sb("pick1", [P, E])
        whalf = sb("whalf", [P, 2, E])
        eth = sb("eth", [P, CHUNKS, 512])
        eg = eth
        esum = sb("esum", [P, 512])
        comb = sb("comb", [P, D])
        combT = sb("combT", [P, H, P])
        yss = sb("yss", [P, 1])
        yve = sb("yve", [P, 1])
        yrms = sb("yrms", [P, 1])
        ynw = sb("ynw", [P, D])
        ysq = sb("ysq", [P, D])
        x2 = sb("x2", [P, D])
        x3 = sb("x3", [P, 2, D])
        ast = sb("ast", [P, 6])
        amv = sb("amv", [P, 2])
        ave = sb("ave", [P, 1])
        arstd = sb("arstd", [P, 1])
        bst = sb("bst", [P, 6])
        bmv = sb("bmv", [P, 2])
        bve = sb("bve", [P, 1])
        brstd = sb("brstd", [P, 1])
        xn2 = sb("xn2", [P, D])
        xn2T = sb("xn2T", [P, H, P])
        xn3 = sb("xn3", [P, D])
        xn3T = sb("xn3T", [P, H, P])
        h1 = sb("h1", [P, H, P])
        lg2 = sb("lg2", [P, K])
        lmax = sb("lmax", [P, 1])
        alpha = sb("alpha", [P, K])
        lsum = sb("lsum", [P, 1])
        lrec = sb("lrec", [P, 1])
        avx = sb("avx", [P, K, R])
        avxT = sb("avxT", [P, KT, P])
        xout = sb("xout", [P, 2, D])

        ew_raw = Brep[:, 1, :]
        convW = cst["conv_w"].rearrange("p (j e) -> p j e", j=DC)

        dA = [ps("dA0"), ps("dA1")]
        hT = ps("hT")
        hE = [ps("hE0"), ps("hE1")]
        pA = ps("pA")
        pB = ps("pB")
        pP = ps("pP")
        B_rows = nc.dram_tensor("B_rows", [B, DS * L], F32, kind="Internal").ap()

        early_in, late_in, ctx_in, x_in = sem("early_in"), sem("late_in"), sem("ctx_in"), sem("x_in")
        experts_in, expert_b_in = sem("experts_in"), sem("expert_b_in")
        zeroed, const_v, const_a = sem("zeroed"), sem("const_v"), sem("const_a")
        experts_hi, experts_split, bias_split, router_split, eb_rows_in = (
            sem(n) for n in ("experts_hi", "experts_split", "bias_split", "router_split", "eb_rows_in"))
        g_stats, g_mv, g_ve, g_rstd, zn_done, zT_done = (sig(n) for n in ("g_stats", "g_mv", "g_ve", "g_rstd", "zn_done", "zT_done"))
        zth_done, gate_done = sig("zth_done"), sig("gate_done")
        xc_done, uth_done, uhalf_done, u_done = sig("xc_done"), sig("uth_done"), sig("uhalf_done"), sig("u_done")
        dtB_mm, dtB_done, C_mm, C_done = sig("dtB_mm"), sig("dtB_done"), sig("C_mm"), sig("C_done")
        B_out, B_in = sig("B_out", 16), sig("B_in", 16)
        dt_mm, sp_abs_done, sp_exp_done, sp_log_done = sig("dt_mm"), sig("sp_abs_done"), sig("sp_exp_done"), sig("sp_log_done")
        sp_pos_done, delta_done, du_done = sig("sp_pos_done"), sig("delta_done"), sig("du_done")
        skip_mm, y_init = sig("skip_mm"), sig("y_init")
        q_mm, q_done, k_mm, k_done, en_mm = sig("q_mm"), sig("q_done"), sig("k_mm"), sig("k_done"), sig("en_mm")
        amax_done, aexp_done, arec_done, att_done, attT_mm, attT_done = (sig(n) for n in ("amax_done", "aexp_done", "arec_done", "att_done", "attT_mm", "attT_done"))
        dA_done, dBu_done, h_done, hT_done = sig("dA_done", DS), sig("dBu_done", DS), sig("h_done", DS), sig("hT_done", DS)
        y_done = sig("y_done", H * DS)
        gated_done, x1_done = sig("gated_done"), sig("x1_done")
        m_stats, m_mv, m_ve, m_rstd, xn1_done, xn1b_done, xn1T_mm, xh_done, xl_done = (
            sig(n) for n in ("m_stats", "m_mv", "m_ve", "m_rstd", "xn1_done", "xn1b_done", "xn1T_mm", "xh_done", "xl_done"))
        logit_mm, logit_done, top_done, topi_done, topf_done, gap_done, gexp_done, gden_done, w0_done, w1_done = (
            sig(n) for n in ("logit_mm", "logit_done", "top_done", "topi_done", "topf_done", "gap_done", "gexp_done", "gden_done", "w0_done", "w1_done"))
        pick_done, wsum_done, whalf_done = sig("pick_done"), sig("wsum_done"), sig("whalf_done")
        expert_mm, eth_done, eg_done, esum_done = sig("expert_mm", CHUNKS), sig("eth_done", 2 * CHUNKS), sig("eg_done", CHUNKS), sig("esum_done", CHUNKS)
        combT_mm, combT_done, proj_mm, yv_done, yss_done, yve_done, yrms_done, ynw_done, x2_done = (
            sig(n) for n in ("combT_mm", "combT_done", "proj_mm", "yv_done", "yss_done", "yve_done", "yrms_done", "ynw_done", "x2_done"))
        a_stats, a_mv, a_ve, a_rstd, b_stats, b_mv, b_ve, b_rstd = (
            sig(n) for n in ("a_stats", "a_mv", "a_ve", "a_rstd", "b_stats", "b_mv", "b_ve", "b_rstd"))
        xn2_done, xn2T_mm, xn2T_done, xm_mm, x3_done, xn3_done, xn3T_mm, xn3T_done = (
            sig(n) for n in ("xn2_done", "xn2T_mm", "xn2T_done", "xm_mm", "x3_done", "xn3_done", "xn3T_mm", "xn3T_done"))
        h1_mm, h1_done, lg2_mm, lg2_done, lmax_done, alpha_done, lrec_done = (
            sig(n) for n in ("h1_mm", "h1_done", "lg2_mm", "lg2_done", "lmax_done", "alpha_done", "lrec_done"))
        vx_mm, avx_done, avxT_mm, avxT_done = (sig(n) for n in ("vx_mm", "avx_done", "avxT_mm", "avxT_done"))
        o_mm, xout_done = sig("o_mm"), sig("xout_done")
        stored = [sig("stored_even", 16), sig("stored_odd", 16)]

        block = stack.enter_context(nc.Block())

        def run(slot):
            last = max(p if isinstance(p, int) else max(p) for table in WHEN.values() for p in table.values())
            for now in range(UNIT_AT[-1] + last + 1):
                def due(starts, when, k):
                    start = now - (when if isinstance(when, int) else when[k])
                    return starts.index(start) if start in starts else None

                def batch(when, k=0):
                    return due(BATCH_AT, when, k)

                def unit(when, k=0):
                    return due(UNIT_AT, when, k)

                slot(batch, unit)

        @block.sync
        def _(sp):
            at = WHEN["sp"]
            sp.dma_start(early_sb[:, :], early).then_inc(early_in, 16)
            sp.dma_start(ctx[:, :, DC - 1:], ctxT).then_inc(ctx_in, 16)
            sp.dma_start(dtp[:, :], dt_projT).then_inc(early_in, 16)
            sp.dma_start(xin[:, :, :, :], x).then_inc(x_in, 16)
            sp.dma_start(late_sb[:, :], late).then_inc(late_in, 16)
            sp.dma_start(ew_raw, experts).then_inc(experts_in, 16)
            sp.dma_start(eb_raw[:, :], expert_b).then_inc(expert_b_in, 16)

            def slot(batch, unit):
                if (b := batch(at["B_rows"])) is not None:
                    wait(sp, dtB_done, b)
                    sp.dma_start(B_rows[b].rearrange("(n l) -> n l", n=DS), dtB[DR:DR + DS, :]).then_inc(B_out.sem, 16)
                    wait(sp, B_out, b)
                    wait(sp, dBu_done, b - 2)
                    if b == 1:
                        sp.wait_ge(experts_split, PIECES)
                    sp.dma_start(Brep[:, b % 2, :], B_rows[b:b + 1, :].to_broadcast([P, DS * L])).then_inc(B_in.sem, 16)
                if batch(at["eb_rows"]) == 0:
                    sp.wait_ge(bias_split, 2)
                    for k, part in enumerate((eb_hi, eb_lo)):
                        sp.dma_start(eb_rows[k:k + 1, :].bitcast(F32), part[:, :].bitcast(F32)).then_inc(eb_rows_in, 16)
                if (j := unit(at["store"])) is not None:
                    wait(sp, xout_done, j)
                    sp.dma_start(out[:, j // H, j % H], xout[:, j % 2]).then_inc(stored[j % 2].sem, 16)

            run(slot)
            for last in stored:
                wait(sp, last, UNITS // 2 - 1)

        @block.gpsimd
        def _(pool):
            at = WHEN["pool"]
            nc.gpsimd.memset(ctx[:, :, 0:DC - 1], 0.0)
            nc.gpsimd.memset(ones2[:, :], 1.0)
            nc.gpsimd.memset(neg_half[:, :], -0.5).then_inc(zeroed, 1)

            def rsqrt(dst, src, ready, b, k, done):
                wait(pool, ready, b, k)
                nc.gpsimd.tensor_tensor(dst, src, neg_half[:, 0:src.shape[-1]], ALU.pow).then_inc(done.sem, 1)

            def slot(batch, unit):
                if (b := batch(at["g_rstd"])) is not None:
                    wait(pool, zn_done, b - 1)
                    rsqrt(grstd[:, :], gve[:, :], g_ve, b, None, g_rstd)
                if (b := batch(at["du"])) is not None:
                    wait(pool, delta_done, b)
                    wait(pool, u_done, b)
                    wait(pool, dBu_done, b - 2)
                    nc.gpsimd.tensor_tensor(du[:, b % 2], delta[:, b % 2], u[:, :, :], ALU.mult).then_inc(du_done.sem, 1)
                for n in range(DS):
                    if (b := batch(at["dBu"], n)) is None:
                        continue
                    if n == 0:
                        wait(pool, B_in, b)
                        wait(pool, du_done, b)
                    if n >= 2:
                        wait(pool, h_done, b, n - 1)
                    else:
                        wait(pool, h_done, b - 1, DS - 1 + n)
                    nc.gpsimd.tensor_tensor(
                        dBu[:, n % 2], du[:, b % 2],
                        Brep[:, b % 2, n * L:(n + 1) * L].unsqueeze(1).to_broadcast([P, H, L]), ALU.mult).then_inc(dBu_done.sem, 1)
                if (j := unit(at["m_rstd"])) is not None:
                    wait(pool, xn1_done, j - 1)
                    rsqrt(mrstd[:, :], mve[:, :], m_ve, j, None, m_rstd)
                if (j := unit(at["xn1b"])) is not None:
                    if j == 0:
                        pool.wait_ge(late_in, 16)
                    wait(pool, xn1_done, j)
                    wait(pool, ynw_done, j - 2)
                    nc.gpsimd.tensor_tensor(xn1b[:, j % 2], xn1[:, :], cst["proj_b"], ALU.add).then_inc(xn1b_done.sem, 1)
                if (j := unit(at["esum"], 0)) is not None:
                    wait(pool, eg_done, j, 2)
                    wait(pool, esum_done, j - 1)
                    nc.gpsimd.tensor_tensor(esum[:, :], eg[:, 0], eg[:, 1], ALU.add).then_inc(esum_done.sem, 1)
                for c in range(2, CHUNKS):
                    if (j := unit(at["esum"], c - 1)) is None:
                        continue
                    wait(pool, eg_done, j, c + 1)
                    wait(pool, esum_done, j, c - 1)
                    nc.gpsimd.tensor_tensor(esum[:, :], esum[:, :], eg[:, c], ALU.add).then_inc(esum_done.sem, 1)
                if (j := unit(at["comb"])) is not None:
                    wait(pool, esum_done, j, 3)
                    wait(pool, combT_mm, j - 1)
                    nc.gpsimd.tensor_tensor(comb[:, :], esum[:, 0:D], esum[:, D:], ALU.add).then_inc(esum_done.sem, 1)
                if (j := unit(at["yrms"])) is not None:
                    wait(pool, ynw_done, j - 1)
                    rsqrt(yrms[:, :], yve[:, :], yve_done, j, None, yrms_done)
                if (j := unit(at["a_rstd"])) is not None:
                    wait(pool, xn2_done, j - 1)
                    rsqrt(arstd[:, :], ave[:, :], a_ve, j, None, a_rstd)
                if (j := unit(at["b_rstd"])) is not None:
                    wait(pool, xn3_done, j - 1)
                    rsqrt(brstd[:, :], bve[:, :], b_ve, j, None, b_rstd)

            pool.wait_ge(zeroed, 1)
            run(slot)

        @block.scalar
        def _(act):
            at = WHEN["act"]
            fn = nc.scalar.activation
            act.wait_ge(early_in, 32)
            fn(negA[:, :], cst["A_log"], ACT.Exp).then_inc(const_a, 1)
            act.wait_ge(const_v, 1)

            def slot(batch, unit):
                if (b := batch(at["uth"])) is not None:
                    wait(act, xc_done, b)
                    wait(act, gate_done, b - 1)
                    for h in range(H):
                        i = fn(uth[:, h], halves(pP[:, :])[:, h], ACT.Tanh, bias=half_cb[:, h:h + 1], scale=0.5)
                    i.then_inc(uth_done.sem, 1)
                if (b := batch(at["dtB"])) is not None:
                    wait(act, C_mm, b)
                    wait(act, B_out, b - 1)
                    wait(act, dt_mm, b - 1)
                    fn(dtB[:, :], pP[0:DR + DS, 0:L], ACT.Copy).then_inc(dtB_done.sem, 1)
                if (b := batch(at["C"])) is not None:
                    wait(act, C_mm, b)
                    wait(act, y_done, b - 2)
                    fn(Ct[:, b % 2], pP[:, L:L + H * DS].rearrange("p (h n) -> p h n", h=H), ACT.Copy).then_inc(C_done.sem, 1)
                if (b := batch(at["sp_abs"])) is not None:
                    wait(act, dt_mm, b)
                    wait(act, delta_done, b - 1)
                    for h in range(H):
                        i = fn(sp_abs[:, h], halves(pP[:, :])[:, h], ACT.Abs, bias=cst["dt_b"][:, h:h + 1])
                    i.then_inc(sp_abs_done.sem, 1)
                if (b := batch(at["sp_exp"])) is not None:
                    wait(act, sp_abs_done, b)
                    fn(sp_exp[:, :, :], sp_abs[:, :, :], ACT.Exp, scale=-1.0).then_inc(sp_exp_done.sem, 1)
                if (b := batch(at["sp_log"])) is not None:
                    wait(act, sp_exp_done, b)
                    fn(sp_log[:, :, :], sp_exp[:, :, :], ACT.Ln, bias=1.0).then_inc(sp_log_done.sem, 1)
                if (b := batch(at["y_init"])) is not None:
                    wait(act, skip_mm, b)
                    wait(act, x1_done, b - 2)
                    fn(y[:, b % 2], halves(pP[:, :]), ACT.Copy).then_inc(y_init.sem, 1)
                if (b := batch(at["zth"])) is not None:
                    wait(act, zT_done, b)
                    wait(act, u_done, b)
                    fn(zth[:, :, :], halves(pP[:, :]), ACT.Tanh, scale=0.5).then_inc(zth_done.sem, 1)
                if (b := batch(at["experts_hi"])) is not None and b == 0:
                    act.wait_ge(experts_in, 16)
                    fn(ew_hi[:, :, :], ew_raw.rearrange("p (h c) -> p h c", h=H), ACT.Copy).then_inc(experts_hi, 1)
                if (b := batch(at["q"])) is not None:
                    wait(act, q_mm, b)
                    wait(act, en_mm, b - 1)
                    fn(qT[:, :], pP[:, 0:L], ACT.Identity, bias=cst["bq"]).then_inc(q_done.sem, 1)
                    fn(kT[:, :], pP[:, L:2 * L], ACT.Identity, bias=cst["bk"]).then_inc(k_done.sem, 1)
                if (b := batch(at["aexp"])) is not None:
                    wait(act, amax_done, b)
                    wait(act, attT_mm, b - 1)
                    for h in range(H):
                        i = fn(aexp[:, h], halves(pP[:, :])[:, h], ACT.Exp, bias=amax[:, h:h + 1], accum_out=asum[:, h:h + 1])
                    i.then_inc(aexp_done.sem, 1)
                if (b := batch(at["attT"])) is not None:
                    wait(act, attT_mm, b)
                    wait(act, xm_mm, H * (b - 3) + H - 1)
                    fn(attT[:, b % 3], halves(pP[:, :]), ACT.Copy).then_inc(attT_done.sem, 1)
                for n in range(DS):
                    if (b := batch(at["dA"], n)) is None:
                        continue
                    if n == 0:
                        wait(act, delta_done, b)
                    if n >= 2:
                        wait(act, h_done, b, n - 1)
                    else:
                        wait(act, h_done, b - 1, DS - 1 + n)
                    for h in range(H):
                        i = fn(halves(dA[n % 2][:, :])[:, h, 1:], delta[:, b % 2, h, 1:], ACT.Exp,
                               scale=negA_n[:, h * DS + n:h * DS + n + 1])
                    i.then_inc(dA_done.sem, 1)

                def silu_part(j, c):
                    wait(act, expert_mm, j, c + 1)
                    wait(act, esum_done, j - 1)
                    fn(eth[:, c], hE[(c + 1) % 2][:, :], ACT.Tanh, scale=0.5).then_inc(eth_done.sem, 1)
                    wait(act, eth_done, j, 2 * c + 1)
                    wait(act, whalf_done, j)
                    for k in range(2):
                        w = whalf[:, j % 2, 2 * c + k:2 * c + k + 1]
                        i = fn(eth[:, c, k * D:(k + 1) * D], eth[:, c, k * D:(k + 1) * D], ACT.Identity, scale=w, bias=w)
                    i.then_inc(eth_done.sem, 1)

                if (j := unit(at["xh"])) is not None:
                    wait(act, xn1T_mm, j)
                    wait(act, expert_mm, j - 1)
                    fn(xh[:, :, :], halves(hE[0][:, 0:D]), ACT.Copy).then_inc(xh_done.sem, 1)
                if (j := unit(at["gexp"])) is not None:
                    wait(act, gap_done, j)
                    wait(act, w1_done, j - 1)
                    fn(gexp[:, :], gap[:, :], ACT.Exp).then_inc(gexp_done.sem, 1)
                for c in range(CHUNKS):
                    if (j := unit(at["silu"], c)) is not None:
                        silu_part(j, c)
                if (j := unit(at["combT"])) is not None:
                    wait(act, combT_mm, j)
                    wait(act, proj_mm, j - 1)
                    fn(combT[:, :, :], halves(pA[:, 0:D]), ACT.Copy).then_inc(combT_done.sem, 1)
                if (j := unit(at["yss"])) is not None:
                    wait(act, yv_done, j)
                    wait(act, yve_done, j - 1)
                    wait(act, yss_done, j - 1)
                    fn(ysq[:, :], xn1b[:, j % 2], ACT.Square, accum_out=yss[:, :]).then_inc(yss_done.sem, 1)
                if (j := unit(at["xn2T"])) is not None:
                    wait(act, xn2T_mm, j)
                    wait(act, xm_mm, j - 1)
                    fn(xn2T[:, :, :], halves(pA[:, 0:D]), ACT.Copy).then_inc(xn2T_done.sem, 1)
                if (j := unit(at["xn3T"])) is not None:
                    wait(act, xn3T_mm, j)
                    wait(act, vx_mm, j - 1)
                    fn(xn3T[:, :, :], halves(pB[:, 0:D]), ACT.Copy).then_inc(xn3T_done.sem, 1)
                if (j := unit(at["h1"])) is not None:
                    wait(act, h1_mm, j)
                    wait(act, lg2_mm, j - 1)
                    for h in range(H):
                        i = fn(h1[:, h], halves(pB[:, D:])[:, h], ACT.Relu, bias=cst["b1"][:, h:h + 1])
                    i.then_inc(h1_done.sem, 1)
                if (j := unit(at["alpha"])) is not None:
                    wait(act, lmax_done, j)
                    wait(act, avx_done, j - 1)
                    wait(act, lrec_done, j - 1)
                    fn(alpha[:, :], lg2[:, :], ACT.Exp, bias=lmax[:, :], accum_out=lsum[:, :]).then_inc(alpha_done.sem, 1)
                if (j := unit(at["avxT"])) is not None:
                    wait(act, avxT_mm, j)
                    wait(act, o_mm, j - 1)
                    fn(avxT[:, :, :], pB[:, :].rearrange("p (k c) -> p k c", k=KT), ACT.Copy).then_inc(avxT_done.sem, 1)

            run(slot)

        @block.vector
        def _(dve):
            at = WHEN["dve"]
            v = nc.vector

            def x1_of(j):
                return x1[:, j // H % 2, j % H]

            for bank in dA:
                v.memset(halves(bank[:, :])[:, :, 0:1], 0.0)
            dve.wait_ge(early_in, 32)
            v.tensor_tensor(convW, convW, cst["in_projT"].unsqueeze(1).to_broadcast([P, DC, D]), ALU.mult)
            v.tensor_scalar(half_cb[:, :], cst["conv_b"], 0.5, None, ALU.mult)
            for h in range(H):
                v.tensor_scalar(diagD[:, h], ident, cst["Dskip"][:, h:h + 1], None, ALU.mult)
            dve.wait_ge(const_a, 1)
            v.tensor_scalar(negA_n[:, :], negA[:, :], -1.0, None, ALU.mult).then_inc(const_v, 1)

            def split_experts(k):
                n = H * E * D // PIECES
                v.tensor_tensor(ew_lo_f[:, k * n:(k + 1) * n], ew_raw[:, k * n:(k + 1) * n],
                                ew_hi_f[:, k * n:(k + 1) * n], ALU.subtract).then_inc(experts_split, 1)

            def split_small():
                dve.wait_ge(late_in, 16)
                dve.wait_ge(expert_b_in, 16)
                dve.wait_ge(zeroed, 1)
                v.tensor_copy(ones2r[:, :], ones2[:, :])
                router = halves(cst["router"])
                v.tensor_copy(rw_hi[:, :, :], router).then_inc(router_split, 1)
                v.tensor_copy(eb_hi[:, :], eb_raw[:, :]).then_inc(bias_split, 1)
                dve.wait_ge(router_split, 1)
                v.tensor_tensor(rw_lo[:, :, :], router, rw_hi[:, :, :].bitcast(F32), ALU.subtract).then_inc(router_split, 1)
                dve.wait_ge(bias_split, 1)
                v.tensor_tensor(eb_lo[:, :], eb_raw[:, :], eb_hi[:, :].bitcast(F32), ALU.subtract).then_inc(bias_split, 1)

            def stats_unit(src, st, mv, ve, s_stats, s_mv, s_ve, j):
                v.bn_stats(st[:, :], src).then_inc(s_stats.sem, 1)
                wait(dve, s_stats, j)
                v.bn_aggr(mv[:, :], st[:, :]).then_inc(s_mv.sem, 1)
                wait(dve, s_mv, j)
                v.tensor_scalar(ve[:, :], mv[:, 1:2], 1e-5, None, ALU.add).then_inc(s_ve.sem, 1)

            def normalize_unit(dst, src, mv, rstd, s_rstd, j, done):
                wait(dve, s_rstd, j)
                v.tensor_scalar(dst, src, mv[:, 0:1], rstd[:, :], ALU.subtract, ALU.mult).then_inc(done.sem, 1)

            def weighted_silu(j, c):
                wait(dve, eth_done, j, 2 * c + 2)
                v.tensor_tensor(eg[:, c], hE[(c + 1) % 2][:, :], eth[:, c], ALU.mult).then_inc(eg_done.sem, 1)

            def stats(src, st, mv, ve, eps, s_stats, s_mv, s_ve, b, k):
                for h in range(H):
                    i = v.bn_stats(st[:, h], src[:, h])
                i.then_inc(s_stats.sem, 1)
                wait(dve, s_stats, b, k)
                for h in range(H):
                    i = v.bn_aggr(mv[:, h], st[:, h])
                i.then_inc(s_mv.sem, 1)
                wait(dve, s_mv, b, k)
                v.tensor_scalar(ve, mv[:, :, 1], eps, None, ALU.add).then_inc(s_ve.sem, 1)

            def normalize(dst, src, mv, rstd, s_rstd, b, k, done):
                wait(dve, s_rstd, b, k)
                for h in range(H):
                    i = v.tensor_scalar(dst[:, h], src[:, h], mv[:, h, 0:1], rstd[:, h:h + 1], ALU.subtract, ALU.mult)
                i.then_inc(done.sem, 1)

            def slot(batch, unit):
                if (b := batch(at["g_stats"])) is not None:
                    if b == 0:
                        dve.wait_ge(x_in, 16)
                    stats(xin[:, b], gst, gmv, gve[:, :], 1e-5, g_stats, g_mv, g_ve, b, None)
                if (b := batch(at["uhalf"])) is not None:
                    wait(dve, uth_done, b)
                    wait(dve, delta_done, b - 1)
                    for h in range(H):
                        i = v.tensor_scalar(uhalf[:, h], halves(pP[:, :])[:, h], cst["conv_b"][:, h:h + 1], 0.5, ALU.add, ALU.mult)
                    i.then_inc(uhalf_done.sem, 1)
                if (b := batch(at["u"])) is not None:
                    wait(dve, uhalf_done, b)
                    wait(dve, du_done, b - 1)
                    wait(dve, skip_mm, b - 1)
                    v.scalar_tensor_tensor(u[:, :, :], uth[:, :, :], 1.0, uhalf[:, :, :], ALU.add, ALU.mult).then_inc(u_done.sem, 1)
                if (b := batch(at["zn"])) is not None:
                    wait(dve, zT_done, b - 1)
                    normalize(zn, xin[:, b], gmv, grstd, g_rstd, b, None, zn_done)
                if (b := batch(at["sp_pos"])) is not None:
                    wait(dve, sp_abs_done, b)
                    for h in range(H):
                        i = v.tensor_scalar(sp_pos[:, h], halves(pP[:, :])[:, h], cst["dt_b"][:, h:h + 1], 0.0, ALU.add, ALU.max)
                    i.then_inc(sp_pos_done.sem, 1)
                if (b := batch(at["delta"])) is not None:
                    wait(dve, sp_pos_done, b)
                    wait(dve, sp_log_done, b)
                    wait(dve, dA_done, b - 2)
                    v.tensor_tensor(delta[:, b % 2], sp_pos[:, :, :], sp_log[:, :, :], ALU.add).then_inc(delta_done.sem, 1)
                if (b := batch(at["gate"])) is not None:
                    wait(dve, zth_done, b)
                    wait(dve, gated_done, b - 2)
                    v.scalar_tensor_tensor(gate[:, b % 2], zth[:, :, :], 1.0, halves(pP[:, :]), ALU.add, ALU.mult).then_inc(gate_done.sem, 1)
                if (b := batch(at["split_small"])) is not None and b == 0:
                    split_small()
                    dve.wait_ge(experts_hi, 1)
                    for k in range(PIECES // 2):
                        split_experts(k)
                for k in range(PIECES // 2):
                    if batch(at["split_experts"], k) == 0:
                        dve.wait_ge(experts_hi, 1)
                        split_experts(PIECES // 2 + k)
                if (b := batch(at["amax"])) is not None:
                    wait(dve, en_mm, b)
                    wait(dve, aexp_done, b - 1)
                    v.tensor_reduce(amax[:, :], halves(pP[:, :]), AX.X, ALU.max, negate=True).then_inc(amax_done.sem, 1)
                if (b := batch(at["arec"])) is not None:
                    wait(dve, aexp_done, b)
                    v.reciprocal(arec[:, :], asum[:, :]).then_inc(arec_done.sem, 1)
                    wait(dve, arec_done, b)
                    for h in range(H):
                        i = v.tensor_scalar(att[:, h], aexp[:, h], arec[:, h:h + 1], None, ALU.mult)
                    i.then_inc(att_done.sem, 1)
                for n in range(DS):
                    if (b := batch(at["scan"], n)) is None:
                        continue
                    wait(dve, dA_done, b, n + 1)
                    wait(dve, dBu_done, b, n + 1)
                    if n >= 2:
                        wait(dve, hT_done, b, n - 1)
                    else:
                        wait(dve, hT_done, b - 1, DS - 1 + n)
                    v.tensor_tensor_scan(out=hst[:, n % 2].rearrange("p h l -> p (h l)"), data0=dA[n % 2][:, :],
                                         data1=dBu[:, n % 2].rearrange("p h l -> p (h l)"), initial=0.0,
                                         op0=ALU.mult, op1=ALU.add).then_inc(h_done.sem, 1)
                for n in range(DS):
                    if (b := batch(at["y"], n)) is None:
                        continue
                    if n == 0:
                        wait(dve, y_init, b)
                        wait(dve, C_done, b)
                    wait(dve, hT_done, b, n + 1)
                    for h in range(H):
                        if n:
                            wait(dve, y_done, b, H * (n - 1) + h + 1)
                        v.scalar_tensor_tensor(y[:, b % 2, h], halves(hT[:, :])[:, h], Ct[:, b % 2, h, n:n + 1],
                                               y[:, b % 2, h], ALU.mult, ALU.add).then_inc(y_done.sem, 1)
                if (b := batch(at["x1"])) is not None:
                    wait(dve, y_done, b)
                    wait(dve, gate_done, b)
                    v.scalar_tensor_tensor(y[:, b % 2], y[:, b % 2], 0.5, gate[:, b % 2], ALU.mult, ALU.mult).then_inc(gated_done.sem, 1)
                    wait(dve, gated_done, b)
                    wait(dve, x2_done, H * (b - 2) + H - 1)
                    v.tensor_tensor(x1[:, b % 2], y[:, b % 2], xin[:, b], ALU.add).then_inc(x1_done.sem, 1)
                if (j := unit(at["m_stats"])) is not None:
                    wait(dve, x1_done, j // H)
                    stats_unit(x1_of(j), mst, mmv, mve, m_stats, m_mv, m_ve, j)
                if (j := unit(at["xn1"])) is not None:
                    wait(dve, xn1b_done, j - 1)
                    wait(dve, xn1T_mm, j - 1)
                    normalize_unit(xn1[:, :], x1_of(j), mmv, mrstd, m_rstd, j, xn1_done)
                if (j := unit(at["xl"])) is not None:
                    wait(dve, xh_done, j)
                    v.tensor_tensor(xl[:, :, :], halves(hE[0][:, 0:D]), xh[:, :, :].bitcast(F32), ALU.subtract).then_inc(xl_done.sem, 1)
                if (j := unit(at["logit"])) is not None:
                    wait(dve, logit_mm, j)
                    v.tensor_tensor(logit[:, :], hE[0][:, D:D + E], cst["router_b"], ALU.add).then_inc(logit_done.sem, 1)
                    wait(dve, logit_done, j)
                    v.max(top[:, :], logit[:, :]).then_inc(top_done.sem, 1)
                    wait(dve, top_done, j)
                    v.tensor_tensor(gap[:, :], top[:, 1:2], top[:, 0:1], ALU.subtract).then_inc(gap_done.sem, 1)
                    v.max_index(topi[:, :], top[:, :], logit[:, :]).then_inc(topi_done.sem, 1)
                    wait(dve, topi_done, j)
                    v.tensor_copy(topf[:, :], topi[:, :]).then_inc(topf_done.sem, 1)
                if (j := unit(at["gden"])) is not None:
                    wait(dve, gexp_done, j)
                    v.tensor_scalar(gden[:, :], gexp[:, :], 1.0, None, ALU.add).then_inc(gden_done.sem, 1)
                    wait(dve, gden_done, j)
                    v.reciprocal(w0[:, :], gden[:, :]).then_inc(w0_done.sem, 1)
                    wait(dve, w0_done, j)
                    v.tensor_tensor(w1[:, :], gexp[:, :], w0[:, :], ALU.mult).then_inc(w1_done.sem, 1)
                    wait(dve, w1_done, j)
                    v.tensor_scalar(pick0[:, :], cst["iota"], topf[:, 0:1], w0[:, :], ALU.is_equal, ALU.mult)
                    v.tensor_scalar(pick1[:, :], cst["iota"], topf[:, 1:2], w1[:, :], ALU.is_equal, ALU.mult).then_inc(pick_done.sem, 1)
                    wait(dve, pick_done, j)
                    wait(dve, eth_done, j - 2)
                    v.tensor_tensor(whalf[:, j % 2, :], pick0[:, :], pick1[:, :], ALU.add).then_inc(wsum_done.sem, 1)
                    wait(dve, wsum_done, j)
                    v.tensor_scalar(whalf[:, j % 2, :], whalf[:, j % 2, :], 0.5, None, ALU.mult).then_inc(whalf_done.sem, 1)
                for c in range(CHUNKS):
                    if (j := unit(at["eg"], c)) is not None:
                        weighted_silu(j, c)
                if (j := unit(at["yv"])) is not None:
                    wait(dve, proj_mm, j)
                    wait(dve, xn1b_done, j)
                    v.tensor_tensor(xn1b[:, j % 2], pA[:, D:], xn1b[:, j % 2], ALU.add).then_inc(yv_done.sem, 1)
                if (j := unit(at["yve"])) is not None:
                    wait(dve, yss_done, j)
                    wait(dve, yrms_done, j - 1)
                    v.tensor_scalar(yve[:, :], yss[:, :], 1.0 / D, 1e-6, ALU.mult, ALU.add).then_inc(yve_done.sem, 1)
                if (j := unit(at["ynw"])) is not None:
                    wait(dve, yrms_done, j)
                    v.scalar_tensor_tensor(ynw[:, :], xn1b[:, j % 2], yrms[:, :], cst["norm_w"], ALU.mult, ALU.mult).then_inc(ynw_done.sem, 1)
                    wait(dve, ynw_done, j)
                    wait(dve, x3_done, j - 1)
                    v.tensor_tensor(x2[:, :], ynw[:, :], x1_of(j), ALU.add).then_inc(x2_done.sem, 1)
                    wait(dve, x2_done, j)
                    stats_unit(x2[:, :], ast, amv, ave, a_stats, a_mv, a_ve, j)
                if (j := unit(at["xn2"])) is not None:
                    wait(dve, xn2T_mm, j - 1)
                    normalize_unit(xn2[:, :], x2[:, :], amv, arstd, a_rstd, j, xn2_done)
                if (j := unit(at["x3"])) is not None:
                    wait(dve, xm_mm, j)
                    wait(dve, xout_done, j - 2)
                    v.tensor_tensor(x3[:, j % 2], pA[:, D:], x2[:, :], ALU.add).then_inc(x3_done.sem, 1)
                    wait(dve, x3_done, j)
                    stats_unit(x3[:, j % 2], bst, bmv, bve, b_stats, b_mv, b_ve, j)
                if (j := unit(at["xn3"])) is not None:
                    wait(dve, xn3T_mm, j - 1)
                    normalize_unit(xn3[:, :], x3[:, j % 2], bmv, brstd, b_rstd, j, xn3_done)
                if (j := unit(at["lg2"])) is not None:
                    wait(dve, lg2_mm, j)
                    wait(dve, alpha_done, j - 1)
                    v.tensor_tensor(lg2[:, :], pB[:, 0:K], cst["b2"], ALU.add).then_inc(lg2_done.sem, 1)
                    wait(dve, lg2_done, j)
                    v.tensor_reduce(lmax[:, :], lg2[:, :], AX.X, ALU.max, negate=True).then_inc(lmax_done.sem, 1)
                if (j := unit(at["avx"])) is not None:
                    wait(dve, vx_mm, j)
                    wait(dve, alpha_done, j)
                    wait(dve, avxT_mm, j - 1)
                    v.tensor_tensor(avx[:, :, :], pB[:, :].rearrange("p (k r) -> p k r", k=K),
                                    alpha[:, :].unsqueeze(2).to_broadcast([P, K, R]), ALU.mult).then_inc(avx_done.sem, 1)
                    wait(dve, xout_done, j - 1)
                    v.reciprocal(lrec[:, :], lsum[:, :]).then_inc(lrec_done.sem, 1)
                if (j := unit(at["xout"])) is not None:
                    wait(dve, o_mm, j)
                    wait(dve, lrec_done, j)
                    wait(dve, stored[j % 2], j // 2 - 1)
                    v.scalar_tensor_tensor(xout[:, j % 2], pB[:, 0:D], lrec[:, :], x3[:, j % 2], ALU.mult, ALU.add).then_inc(xout_done.sem, 1)

            run(slot)

        @block.tensor
        def _(pe):
            at = WHEN["pe"]
            def mm(out_, lhsT, rhs, first, last, **kw):
                return nc.tensor.matmul(out_, lhsT, rhs, start=first, stop=last, **kw)

            def transposes(dst, src):
                for j in range(H):
                    for i in range(H):
                        last = nc.tensor.transpose(halves(dst)[:, j, i * P:(i + 1) * P], src[:, i, j * P:(j + 1) * P], ident)
                return last

            def slot(batch, unit):
                if (b := batch(at["xc"])) is not None:
                    if b == 0:
                        pe.wait_ge(ctx_in, 16)
                        pe.wait_ge(zeroed, 1)
                        pe.wait_ge(const_v, 1)
                    wait(pe, gate_done, b - 1)
                    wait(pe, attT_done, b - 2)
                    for h in range(H):
                        for j in range(DC):
                            i = mm(halves(pP[:, :])[:, h], convW[:, j, h * P:(h + 1) * P], ctx[:, b, j:j + L], j == 0, j == DC - 1)
                    i.then_inc(xc_done.sem, 1)
                if (b := batch(at["dtB"])) is not None:
                    wait(pe, u_done, b)
                    for h in range(H):
                        i = mm(pP[0:DR + DS, 0:L], xproj[:, h, 0:DR + DS], u[:, h], h == 0, h == H - 1)
                    i.then_inc(dtB_mm.sem, 1)
                    for g in range(H):
                        for h in range(H):
                            i = mm(pP[:, L + g * DS:L + (g + 1) * DS], u[:, h, g * P:(g + 1) * P], xproj[:, h, DR + DS:], h == 0, h == H - 1)
                    i.then_inc(C_mm.sem, 1)
                if (b := batch(at["dt"])) is not None:
                    wait(pe, dtB_done, b)
                    wait(pe, C_done, b)
                    for h in range(H):
                        i = mm(halves(pP[:, :])[:, h], dtp[:, h * P:(h + 1) * P], dtB[0:DR, :], True, True)
                    i.then_inc(dt_mm.sem, 1)
                if (b := batch(at["skip"])) is not None:
                    wait(pe, sp_abs_done, b)
                    wait(pe, sp_pos_done, b)
                    for g in range(H):
                        for h in range(H):
                            i = mm(halves(pP[:, :])[:, g, h * P:(h + 1) * P], u[:, h, g * P:(g + 1) * P], diagD[:, h], True, True)
                    i.then_inc(skip_mm.sem, 1)
                if (b := batch(at["zT"])) is not None:
                    wait(pe, y_init, b)
                    wait(pe, zn_done, b)
                    transposes(pP[:, :], zn).then_inc(zT_done.sem, 1)
                if (b := batch(at["q"])) is not None:
                    if b == 0:
                        pe.wait_ge(late_in, 16)
                    wait(pe, gate_done, min(b + 1, B - 1))
                    wait(pe, attT_done, b - 1)
                    mm(pP[:, 0:L], cst["WqT"], ctx[:, b, DC - 1:], True, True)
                    mm(pP[:, L:2 * L], cst["WkT"], ctx[:, b, DC - 1:], True, True).then_inc(q_mm.sem, 1)
                if (b := batch(at["en"])) is not None:
                    wait(pe, q_done, b)
                    wait(pe, k_done, b)
                    for h in range(H):
                        i = mm(halves(pP[:, :])[:, h], qT[:, h * P:(h + 1) * P], kT[:, :], True, True)
                    i.then_inc(en_mm.sem, 1)
                if (b := batch(at["attT"])) is not None:
                    wait(pe, att_done, b)
                    transposes(pP[:, :], att).then_inc(attT_mm.sem, 1)
                for n in range(DS):
                    if (b := batch(at["hT"], n)) is None:
                        continue
                    wait(pe, h_done, b, n + 1)
                    wait(pe, y_done, b if n else b - 1, H * n if n else None)
                    transposes(hT[:, :], hst[:, n % 2]).then_inc(hT_done.sem, 1)

                def transposes_unit(dst, src):
                    for h in range(src.shape[-1] // P):
                        last = nc.tensor.transpose(dst[:, h * P:(h + 1) * P], src[:, h * P:(h + 1) * P], ident)
                    return last

                if (j := unit(at["xn1T"])) is not None:
                    wait(pe, xn1_done, j)
                    wait(pe, eg_done, j - 1)
                    transposes_unit(hE[0], xn1).then_inc(xn1T_mm.sem, 1)
                if (j := unit(at["logit"])) is not None:
                    if j == 0:
                        pe.wait_ge(router_split, 2)
                    wait(pe, xl_done, j)
                    n = 0
                    for h in range(H):
                        for a, w in ((xh, rw_hi), (xl, rw_hi), (xh, rw_lo)):
                            i = mm(hE[0][:, D:D + E], a[:, h], w[:, h], n == 0, n == 3 * H - 1)
                            n += 1
                    i.then_inc(logit_mm.sem, 1)
                for c in range(CHUNKS):
                    if (j := unit(at["expert"], c)) is None:
                        continue
                    if c == 0:
                        if j == 0:
                            pe.wait_ge(experts_split, PIECES)
                            pe.wait_ge(eb_rows_in, 32)
                        wait(pe, xl_done, j)
                        wait(pe, eg_done, j - 1, CHUNKS - 1)
                    if c == 1:
                        wait(pe, logit_done, j)
                    if c >= 2:
                        wait(pe, eg_done, j, c - 1)
                    cols = slice(c * 2 * D, (c + 1) * 2 * D)
                    bank = hE[(c + 1) % 2]
                    for h in range(H):
                        for n, (a, w) in enumerate(((xh, ew_hi), (xl, ew_hi), (xh, ew_lo))):
                            mm(bank[:, :], a[:, h], w[:, h, cols], h == 0 and n == 0, False)
                    mm(bank[:, :], ones2r[:, :], eb_rows[:, cols], False, True).then_inc(expert_mm.sem, 1)
                if (j := unit(at["combT"])) is not None:
                    wait(pe, esum_done, j)
                    wait(pe, x3_done, j - 1)
                    transposes_unit(pA, comb).then_inc(combT_mm.sem, 1)
                if (j := unit(at["proj"])) is not None:
                    wait(pe, combT_done, j)
                    for h in range(H):
                        i = mm(pA[:, D:], combT[:, h], halves(cst["proj"])[:, h], h == 0, h == H - 1)
                    i.then_inc(proj_mm.sem, 1)
                if (j := unit(at["xn2T"])) is not None:
                    wait(pe, xn2_done, j)
                    wait(pe, yv_done, j)
                    transposes_unit(pA, xn2).then_inc(xn2T_mm.sem, 1)
                if (j := unit(at["xm"])) is not None:
                    wait(pe, xn2T_done, j)
                    wait(pe, attT_done, j // H)
                    for h in range(H):
                        i = mm(pA[:, D:], xn2T[:, h], attT[:, j // H % 3, h], h == 0, h == H - 1)
                    i.then_inc(xm_mm.sem, 1)
                if (j := unit(at["xn3T"])) is not None:
                    wait(pe, xn3_done, j)
                    wait(pe, xout_done, j - 1)
                    transposes_unit(pB, xn3).then_inc(xn3T_mm.sem, 1)
                if (j := unit(at["h1"])) is not None:
                    wait(pe, xn3T_done, j)
                    w1v = halves(cst["W1"])
                    for g in range(H):
                        for h in range(H):
                            i = mm(halves(pB[:, D:])[:, g], w1v[:, h, g * P:(g + 1) * P], xn3T[:, h], h == 0, h == H - 1)
                    i.then_inc(h1_mm.sem, 1)
                if (j := unit(at["lg2"])) is not None:
                    wait(pe, h1_done, j)
                    for h in range(H):
                        i = mm(pB[:, 0:K], h1[:, h], halves(cst["W2"])[:, h], h == 0, h == H - 1)
                    i.then_inc(lg2_mm.sem, 1)
                if (j := unit(at["vx"])) is not None:
                    wait(pe, lg2_done, j)
                    for h in range(H):
                        i = mm(pB[:, :], xn3T[:, h], halves(cst["VT"])[:, h], h == 0, h == H - 1)
                    i.then_inc(vx_mm.sem, 1)
                if (j := unit(at["avxT"])) is not None:
                    wait(pe, avx_done, j)
                    transposes_unit(pB, avx[:, :, :].rearrange("p k r -> p (k r)")).then_inc(avxT_mm.sem, 1)
                if (j := unit(at["o"])) is not None:
                    wait(pe, avxT_done, j)
                    ut = cst["UT"].rearrange("p (k d) -> p k d", k=KT)
                    for k in range(KT):
                        i = mm(pB[:, 0:D], avxT[:, k], ut[:, k], k == 0, k == KT - 1)
                    i.then_inc(o_mm.sem, 1)

            run(slot)


def kernel(**inputs):
    import numpy as np
    import concourse.bacc as bacc
    from concourse.bass_utils import run_bass_kernel_spmd

    a = {k: np.asarray(v) for k, v in inputs.items()}

    def halves(m):
        return m.reshape(-1, P, m.shape[1]).transpose(1, 0, 2).reshape(P, -1)

    def everywhere(row):
        return np.broadcast_to(row.reshape(1, -1), (P, row.size))

    laid = {
        "in_projT": a["L0_xattn_in_proj_w"].T, "conv_w": everywhere(a["L0_xattn_conv_w"].T),
        "conv_b": halves(a["L0_xattn_conv_b"][:, None]), "x_projT": halves(a["L0_xattn_x_proj_w"].T),
        "dt_b": halves(a["L0_xattn_dt_proj_b"][:, None]), "Dskip": halves(a["L0_xattn_D"][:, None]),
        "A_log": halves(a["L0_xattn_A_log"]), "ident": np.eye(P, dtype=np.float32),
        "WqT": a["L1_xattn_Wq"].T, "WkT": a["L1_xattn_Wk"].T, "bq": a["L1_xattn_bq"][:, None], "bk": a["L1_xattn_bk"][:, None],
        "router": halves(a["L0_ffn_router_w"]), "router_b": everywhere(a["L0_ffn_router_b"]),
        "proj": halves(a["L0_ffn_proj_w"]), "proj_b": everywhere(a["L0_ffn_proj_b"]), "norm_w": everywhere(a["L0_ffn_norm_w"]),
        "W1": halves(a["L1_ffn_W1"]), "b1": halves(a["L1_ffn_b1"][:, None]), "W2": halves(a["L1_ffn_W2"]),
        "b2": everywhere(a["L1_ffn_b2"]), "VT": halves(a["L1_ffn_V"].reshape(K * R, D).T),
        "UT": halves(a["L1_ffn_U"].transpose(0, 2, 1).reshape(K * R, D)), "iota": everywhere(np.arange(E, dtype=np.float32)),
    }
    arrays = {
        "early": np.concatenate([laid[n] for n, _ in EARLY], axis=1),
        "late": np.concatenate([laid[n] for n, _ in LATE], axis=1),
        "experts": halves(a["L0_ffn_expert_w"].transpose(1, 0, 2).reshape(D, E * D)),
        "expert_b": a["L0_ffn_expert_b"].reshape(P, -1),
        "dt_projT": a["L0_xattn_dt_proj_w"].T,
        "ctxT": a["ctx_1024"].transpose(2, 0, 1),
        "x": a["x"].reshape(B, H, P, D).transpose(2, 0, 1, 3),
    }
    arrays = {k: np.ascontiguousarray(m) for k, m in arrays.items()}
    nc = bacc.Bacc("TRN2", target_bir_lowering=False, num_devices=1)
    args = [nc.dram_tensor(k, m.shape, mybir.dt.from_np(m.dtype), kind="ExternalInput").ap() for k, m in arrays.items()]
    out = nc.dram_tensor("out", (P, B, H, D), F32, kind="ExternalOutput").ap()
    build(nc, *args, out)
    got = run_bass_kernel_spmd(nc, [arrays], core_ids=[0]).results[0]["out"]
    return np.ascontiguousarray(got.transpose(1, 2, 0, 3)).reshape(B, L, D)
```

```python
import concourse.bass as bass
from concourse import mybir
from contextlib import ExitStack

F32 = mybir.dt.float32
F32R = mybir.dt.float32r
U32 = mybir.dt.uint32
ALU = mybir.AluOpType
ACT = mybir.ActivationFunctionType
AX = mybir.AxisListType

P = 128
B, L, D, C = 4, 256, 256, 128
H = D // P
DS, DC, DR = 16, 4, 8
E = 8
K, R = 8, 64
KT = K * R // P
CHUNKS = E // 2
UNITS = B * H
FREED = UNITS - 2 * H
B_PARTS = 4
WARM_UP = 6
PIECES = 8

EARLY = [("in_projT", D), ("conv_w", DC * D), ("conv_b", H), ("x_projT", H * (DR + 2 * DS)), ("dt_b", H),
         ("Dskip", H), ("A_log", H * DS), ("ident", P)]
LATE = [("WqT", P), ("WkT", P), ("bq", 1), ("bk", 1), ("router", H * E), ("router_b", E), ("proj", H * D),
        ("proj_b", D), ("norm_w", D), ("W1", H * D), ("b1", H), ("W2", H * K), ("b2", K), ("VT", H * K * R),
        ("UT", KT * D), ("iota", E)]


WHEN = {
    "sp": {
        "B_rows": 5, "eb_rows": 70, "store": 100, "late": 2, "x": 1,
    },
    "pool": {
        "g_rstd": 5, "du": 11, "dBu": (33, 35, 39, 42, 50, 53, 59, 66, 67, 69, 73, 82, 82, 86, 86, 86), "m_rstd": -15,
        "xn1b": -11, "esum": (9, 19, 19), "comb": 19, "yrms": 33, "a_rstd": 46, "b_rstd": 59, "gden": -1, "x1": 105,
    },
    "act": {
        "uth": 10, "dtB": 22, "C": 21, "sp_abs": 26, "sp_exp": 30, "sp_log": 33, "y_init": 38, "zth": 40,
        "dA": (60, 64, 70, 73, 79, 83, 86, 87, 94, 100, 101, 107, 112, 114, 118, 120), "q": 108, "aexp": 120,
        "attT": 134, "xh": 15, "gexp": 24, "silu": (30, 31, 38, 40), "combT": 54, "yss": 59, "xn2T": 73, "xn3T": 94,
        "h1": 97, "alpha": 105, "avxT": 118, "sp_pos": 26, "att": 123,
    },
    "dve": {
        "g_stats": 29, "u": 18, "zn": 30, "delta": 38, "gate": 47, "split_small": 41,
        "scan": (61, 63, 69, 82, 84, 86, 91, 93, 96, 102, 108, 114, 116, 118, 122, 124),
        "y": (73, 80, 83, 85, 89, 92, 93, 99, 109, 111, 114, 116, 119, 123, 124, 126), "amax": 117, "arec": 120,
        "m_stats": 0, "xn1": 14, "xl": 18, "logit": 21, "eg": (29, 30, 46, 47), "yv": 57, "yve": 59, "ynw": 62,
        "xn2": 77, "x3": 83, "xn3": 90, "lg2": 103, "avx": 113, "xout": 123, "m_mv": 4, "m_ve": 10, "a_stats": 68,
        "a_mv": 70, "a_ve": 72, "b_stats": 86, "b_mv": 87, "b_ve": 88, "x2": 66, "top": 22, "gap": 24, "topf": 25,
        "lmax": 105, "lrec": 120, "experts_hi": (18, 20, 21, 25, 26, 26, 29, 61),
        "experts_lo": (45, 59, 61, 63, 66, 69, 71, 79), "gated": 126,
    },
    "pe": {
        "xc": 14, "dtB": 21, "dt": 25, "skip": 36, "zT": 45,
        "hT": (71, 80, 82, 86, 91, 94, 98, 99, 106, 110, 112, 117, 122, 124, 127, 130), "q": 111, "en": 117,
        "attT": 131, "xn1T": 18, "logit": 22, "expert": (28, 32, 35, 44), "combT": 56, "proj": 59, "xn2T": 78,
        "xm": 80, "xn3T": 95, "h1": 98, "lg2": 105, "vx": 109, "avxT": 114, "o": 123,
    },
}

WHEN_LAST = {
    "sp": {
       
    },
    "pool": {
        "m_rstd": -12, "xn1b": 13, "esum": (18, 25, 25), "comb": 25, "yrms": 49, "a_rstd": 56, "b_rstd": 80,
        "gden": 5,
    },
    "act": {
        "xh": 18, "gexp": 29, "silu": (33, 36, 44, 46), "combT": 62, "yss": 74, "xn2T": 80, "xn3T": 108, "h1": 110,
        "alpha": 116, "avxT": 140,
    },
    "dve": {
        "m_stats": 9, "xn1": 20, "xl": 24, "logit": 26, "eg": (33, 40, 51, 54), "yv": 67, "yve": 72, "ynw": 75,
        "xn2": 85, "x3": 89, "xn3": 98, "lg2": 120, "avx": 136, "xout": 151, "m_mv": 12, "m_ve": 14, "a_stats": 78,
        "a_mv": 80, "a_ve": 82, "b_stats": 89, "b_mv": 94, "b_ve": 95, "x2": 76, "top": 27, "gap": 28, "topf": 31,
        "lmax": 120, "lrec": 142,
    },
    "pe": {
        "xn1T": 23, "logit": 28, "expert": (30, 35, 44, 47), "combT": 64, "proj": 69, "xn2T": 85, "xm": 87,
        "xn3T": 109, "h1": 113, "lg2": 118, "vx": 139, "avxT": 141, "o": 145,
    },
}

BATCH_AT = (0, 64, 128, 192)
UNIT_AT = (128, 160, 192, 224, 251, 283, 315, 347)


class Signal:

    def __init__(self, handle, per=1):
        self.sem, self.per = handle, per

    def value(self, b, k=None):
        return self.per * b + (self.per if k is None else k)


def wait(engine, signal, b, k=None):
    if b >= 0:
        engine.wait_ge(signal.sem, signal.value(b, k))


def build(nc, early, late, experts, expert_b, dt_projT, ctxT, x, out):
    with ExitStack() as stack:
        def sb(name, shape, dt=F32):
            return stack.enter_context(nc.sbuf_tensor(name, shape, dt))

        def ps(name):
            return stack.enter_context(nc.psum_tensor(name, [P, 512], F32))

        def sem(name):
            return stack.enter_context(nc.semaphore(name))

        def sig(name, per=1):
            return Signal(sem(name), per)

        def halves(t):
            return t.rearrange("p (h c) -> p h c", h=H)

        early_sb = sb("early_sb", [P, sum(n for _, n in EARLY)])
        late_sb = sb("late_sb", [P, sum(n for _, n in LATE)])
        cst = {}
        for tile, table in ((early_sb, EARLY), (late_sb, LATE)):
            at = 0
            for name, n in table:
                cst[name] = tile[:, at:at + n]
                at += n
        ident = cst["ident"]
        xproj = halves(cst["x_projT"])
        dtp = sb("dtp", [DR, D])
        ew_hi = sb("ew_hi", [P, H, E * D], F32R)
        ew_lo = sb("ew_lo", [P, H, E * D], F32R)
        ew_hi_r = ew_hi[:, :, :].rearrange("p h c -> p (h c)")
        ew_lo_r = ew_lo[:, :, :].rearrange("p h c -> p (h c)")
        warm = sb("warm", [P, L])
        rw_hi = sb("rw_hi", [P, H, E], F32R)
        rw_lo = sb("rw_lo", [P, H, E], F32R)
        eb_raw = sb("eb_raw", [P, E * D // P])
        eb_hi = sb("eb_hi", [P, E * D // P], F32R)
        eb_lo = sb("eb_lo", [P, E * D // P], F32R)
        eb_rows = sb("eb_rows", [2, E * D], F32R)
        ones2 = sb("ones2", [2, P])
        ones2r = sb("ones2r", [2, P], F32R)
        negA = sb("negA", [P, H * DS])
        negA_n = sb("negA_n", [P, H * DS])
        half_cb = sb("half_cb", [P, H])
        diagD = sb("diagD", [P, H, P])
        neg_half = sb("neg_half", [P, H])
        neg_one = sb("neg_one", [P, 1])
        ctx = sb("ctx", [P, B, DC - 1 + L])
        xin = sb("xin", [P, B, H, D])
        gst = sb("gst", [P, H, 6])
        gmv = sb("gmv", [P, H, 2])
        gve = sb("gve", [P, H])
        grstd = sb("grstd", [P, H])
        zn = sb("zn", [P, H, L])
        gate = sb("gate", [P, 2, H, D])
        uth = sb("uth", [P, H, L])
        zth = uth
        uhalf = sb("uhalf", [P, H, L])
        u = sb("u", [P, H, L])
        dtB = sb("dtB", [DR + DS, L])
        Ct = sb("Ct", [P, 2, H, DS])
        sp_abs = sb("sp_abs", [P, H, L])
        sp_exp = sp_log = sp_abs
        sp_pos = uhalf
        delta = sb("delta", [P, 2, H, L])
        du = sb("du", [P, 2, H, L])
        Brep = sb("Brep", [P, 2, DS * L])
        y = sb("y", [P, 2, H, D])
        qT = sb("qT", [P, L])
        kT = sb("kT", [P, L])
        amax = sb("amax", [P, H])
        aexp = sb("aexp", [P, H, L])
        asum = sb("asum", [P, H])
        arec = sb("arec", [P, H])
        att = aexp
        attT = sb("attT", [P, 3, H, L])
        dBu = sb("dBu", [P, 2, H, L])
        hst = sb("hst", [P, 2, H, L])
        x1 = sb("x1", [P, 2, H, D])
        mst = sb("mst", [P, 6])
        mmv = sb("mmv", [P, 2])
        mve = sb("mve", [P, 1])
        mrstd = sb("mrstd", [P, 1])
        xn1 = sb("xn1", [P, D])
        xn1b = sb("xn1b", [P, 2, D])
        xh = sb("xh", [P, H, P], F32R)
        xl = sb("xl", [P, H, P], F32R)
        logit = sb("logit", [P, E])
        top = sb("top", [P, 8])
        topi = sb("topi", [P, 8], U32)
        topf = sb("topf", [P, 8])
        gap = sb("gap", [P, 1])
        gexp = sb("gexp", [P, 1])
        gden = sb("gden", [P, 1])
        w0 = sb("w0", [P, 1])
        w1 = sb("w1", [P, 1])
        pick0 = sb("pick0", [P, E])
        pick1 = sb("pick1", [P, E])
        whalf = sb("whalf", [P, 2, E])
        eth = sb("eth", [P, CHUNKS, 512])
        eg = eth
        esum = sb("esum", [P, 512])
        comb = sb("comb", [P, D])
        combT = sb("combT", [P, H, P])
        yss = sb("yss", [P, 1])
        yve = sb("yve", [P, 1])
        yrms = sb("yrms", [P, 1])
        ynw = sb("ynw", [P, D])
        ysq = sb("ysq", [P, D])
        x2 = sb("x2", [P, D])
        x3 = sb("x3", [P, 2, D])
        ast = sb("ast", [P, 6])
        amv = sb("amv", [P, 2])
        ave = sb("ave", [P, 1])
        arstd = sb("arstd", [P, 1])
        bst = sb("bst", [P, 6])
        bmv = sb("bmv", [P, 2])
        bve = sb("bve", [P, 1])
        brstd = sb("brstd", [P, 1])
        xn2 = sb("xn2", [P, D])
        xn2T = sb("xn2T", [P, H, P])
        xn3 = sb("xn3", [P, D])
        xn3T = sb("xn3T", [P, H, P])
        h1 = sb("h1", [P, H, P])
        lg2 = sb("lg2", [P, K])
        lmax = sb("lmax", [P, 1])
        alpha = sb("alpha", [P, K])
        lsum = sb("lsum", [P, 1])
        lrec = sb("lrec", [P, 1])
        avx = sb("avx", [P, K, R])
        avxT = sb("avxT", [P, KT, P])
        xout = sb("xout", [P, 2, D])

        ew_raw = Brep[:, 1, :]
        convW = cst["conv_w"].rearrange("p (j e) -> p j e", j=DC)

        dA = [ps("dA0"), ps("dA1")]
        hT = ps("hT")
        hE = [ps("hE0"), ps("hE1")]
        pA = ps("pA")
        pB = ps("pB")
        pP = ps("pP")

        def bank_a(j):
            return pP if j >= FREED and j % 2 else pA

        def bank_b(j):
            return dA[1] if j >= FREED and j % 2 else pB

        def bank_vx(j):
            return dA[0] if j >= FREED else pB

        B_rows = nc.dram_tensor("B_rows", [B, DS * L], F32, kind="Internal").ap()

        early_in, late_in, ctx_in, x_in, dtp_in = (sem(n) for n in ("early_in", "late_in", "ctx_in", "x_in", "dtp_in"))
        experts_in, expert_b_in = sem("experts_in"), sem("expert_b_in")
        zeroed, warm_ready, conv_ready, const_v, const_a = (sem(n) for n in ("zeroed", "warm_ready", "conv_ready", "const_v", "const_a"))
        experts_hi, experts_split, bias_split, router_split, eb_rows_in = (
            sem(n) for n in ("experts_hi", "experts_split", "bias_split", "router_split", "eb_rows_in"))
        g_stats, g_mv, g_ve, g_rstd, zn_done, zT_done = (sig(n) for n in ("g_stats", "g_mv", "g_ve", "g_rstd", "zn_done", "zT_done"))
        zth_done, gate_done = sig("zth_done"), sig("gate_done")
        xc_done, uhalf_done, u_done = sig("xc_done"), sig("uhalf_done"), sig("u_done")
        dtB_mm, dtB_done, C_mm, C_done = sig("dtB_mm"), sig("dtB_done"), sig("C_mm"), sig("C_done")
        B_out, B_in = sig("B_out", 16), [sig("B_in%d" % k, 16) for k in range(B_PARTS)]
        dt_mm, sp_abs_done, sp_exp_done, sp_log_done = sig("dt_mm"), sig("sp_abs_done"), sig("sp_exp_done"), sig("sp_log_done")
        sp_pos_done, delta_done, du_done = sig("sp_pos_done"), sig("delta_done"), sig("du_done")
        skip_mm, y_init = sig("skip_mm"), sig("y_init")
        q_mm, q_done, k_done, en_mm = sig("q_mm"), sig("q_done"), sig("k_done"), sig("en_mm")
        amax_done, aexp_done, arec_done, att_done, attT_mm, attT_done = (sig(n) for n in ("amax_done", "aexp_done", "arec_done", "att_done", "attT_mm", "attT_done"))
        dA_done, dBu_done, h_done, hT_done = sig("dA_done", DS), sig("dBu_done", DS), sig("h_done", DS), sig("hT_done", DS)
        y_done = sig("y_done", H * DS)
        gated_done, x1_done = sig("gated_done"), sig("x1_done")
        m_stats, m_mv, m_ve, m_rstd, xn1_done, xn1b_done, xn1T_mm, xh_done, xl_done = (
            sig(n) for n in ("m_stats", "m_mv", "m_ve", "m_rstd", "xn1_done", "xn1b_done", "xn1T_mm", "xh_done", "xl_done"))
        logit_mm, logit_done, top_done, topi_done, topf_done, gap_done, gexp_done, gden_done, w0_done, w1_done = (
            sig(n) for n in ("logit_mm", "logit_done", "top_done", "topi_done", "topf_done", "gap_done", "gexp_done", "gden_done", "w0_done", "w1_done"))
        pick_done, whalf_done = sig("pick_done"), sig("whalf_done")
        expert_mm, eth_done, eg_done, esum_done = sig("expert_mm", CHUNKS), sig("eth_done", 2 * CHUNKS), sig("eg_done", CHUNKS), sig("esum_done", CHUNKS)
        combT_mm, combT_done, proj_mm, yv_done, yss_done, yve_done, yrms_done, ynw_done, x2_done = (
            sig(n) for n in ("combT_mm", "combT_done", "proj_mm", "yv_done", "yss_done", "yve_done", "yrms_done", "ynw_done", "x2_done"))
        a_stats, a_mv, a_ve, a_rstd, b_stats, b_mv, b_ve, b_rstd = (
            sig(n) for n in ("a_stats", "a_mv", "a_ve", "a_rstd", "b_stats", "b_mv", "b_ve", "b_rstd"))
        xn2_done, xn2T_mm, xn2T_done, xm_mm, x3_done, xn3_done, xn3T_mm, xn3T_done = (
            sig(n) for n in ("xn2_done", "xn2T_mm", "xn2T_done", "xm_mm", "x3_done", "xn3_done", "xn3T_mm", "xn3T_done"))
        h1_mm, h1_done, lg2_mm, lg2_done, lmax_done, alpha_done, lrec_done = (
            sig(n) for n in ("h1_mm", "h1_done", "lg2_mm", "lg2_done", "lmax_done", "alpha_done", "lrec_done"))
        vx_mm, avx_done, avxT_mm, avxT_done = (sig(n) for n in ("vx_mm", "avx_done", "avxT_mm", "avxT_done"))
        o_mm, xout_done = sig("o_mm"), sig("xout_done")
        stored = [sig("stored_even", 16), sig("stored_odd", 16)]

        block = stack.enter_context(nc.Block())

        def run(engine, slot):
            usual, final = WHEN[engine], {**WHEN[engine], **WHEN_LAST.get(engine, {})}

            def place(when, k):
                return when if isinstance(when, int) else when[k]

            last = max(place(when, -1) for when in [*usual.values(), *final.values()])
            for now in range(UNIT_AT[-1] + last + 1):
                def batch(piece, k=0):
                    start = now - place(usual[piece], k)
                    return BATCH_AT.index(start) if start in BATCH_AT else None

                def unit(piece, k=0):
                    for j in range(UNITS):
                        if now == UNIT_AT[j] + place((final if j >= FREED else usual)[piece], k):
                            return j
                    return None

                slot(batch, unit)

        @block.sync
        def _(sp):
            sp.dma_start(early_sb[:, :], early).then_inc(early_in, 16)
            sp.dma_start(ctx[:, :, DC - 1:], ctxT).then_inc(ctx_in, 16)
            sp.dma_start(dtp[:, :], dt_projT).then_inc(dtp_in, 16)
            sp.dma_start(ew_raw, experts).then_inc(experts_in, 16)

            def slot(batch, unit):
                if (b := batch("B_rows")) is not None:
                    wait(sp, dtB_done, b)
                    sp.dma_start(B_rows[b].rearrange("(n l) -> n l", n=DS), dtB[DR:DR + DS, :]).then_inc(B_out.sem, 16)
                    wait(sp, B_out, b)
                    wait(sp, dBu_done, b - 2)
                    if b == 1:
                        sp.wait_ge(experts_split, PIECES)
                    for k in range(B_PARTS):
                        part = slice(k * DS * L // B_PARTS, (k + 1) * DS * L // B_PARTS)
                        sp.dma_start(Brep[:, b % 2, part], B_rows[b:b + 1, part].to_broadcast([P, DS * L // B_PARTS])).then_inc(B_in[k].sem, 16)
                if batch("x") == 0:
                    sp.dma_start(xin[:, :, :, :], x).then_inc(x_in, 16)
                if batch("late") == 0:
                    sp.dma_start(late_sb[:, :], late).then_inc(late_in, 16)
                    sp.dma_start(eb_raw[:, :], expert_b).then_inc(expert_b_in, 16)
                if batch("eb_rows") == 0:
                    sp.wait_ge(bias_split, 2)
                    for k, part in enumerate((eb_hi, eb_lo)):
                        sp.dma_start(eb_rows[k:k + 1, :].bitcast(F32), part[:, :].bitcast(F32)).then_inc(eb_rows_in, 16)
                if (j := unit("store")) is not None:
                    wait(sp, xout_done, j)
                    sp.dma_start(out[:, j // H, j % H], xout[:, j % 2]).then_inc(stored[j % 2].sem, 16)

            run("sp", slot)
            for last in stored:
                wait(sp, last, UNITS // 2 - 1)

        @block.gpsimd
        def _(pool):
            nc.gpsimd.memset(ctx[:, :, 0:DC - 1], 0.0)
            nc.gpsimd.memset(ones2[:, :], 1.0)
            nc.gpsimd.memset(neg_one[:, :], -1.0)
            nc.gpsimd.memset(neg_half[:, :], -0.5).then_inc(zeroed, 1)

            def rsqrt(dst, src, ready, b, k, done):
                wait(pool, ready, b, k)
                nc.gpsimd.tensor_tensor(dst, src, neg_half[:, 0:src.shape[-1]], ALU.pow).then_inc(done.sem, 1)

            def slot(batch, unit):
                if (b := batch("g_rstd")) is not None:
                    wait(pool, zn_done, b - 1)
                    rsqrt(grstd[:, :], gve[:, :], g_ve, b, None, g_rstd)
                if (b := batch("du")) is not None:
                    wait(pool, delta_done, b)
                    wait(pool, u_done, b)
                    wait(pool, dBu_done, b - 2)
                    nc.gpsimd.tensor_tensor(du[:, b % 2], delta[:, b % 2], u[:, :, :], ALU.mult).then_inc(du_done.sem, 1)
                for n in range(DS):
                    if (b := batch("dBu", n)) is None:
                        continue
                    if n % (DS // B_PARTS) == 0:
                        wait(pool, B_in[n // (DS // B_PARTS)], b)
                    if n == 0:
                        wait(pool, du_done, b)
                    if n >= 2:
                        wait(pool, h_done, b, n - 1)
                    else:
                        wait(pool, h_done, b - 1, DS - 1 + n)
                    nc.gpsimd.tensor_tensor(
                        dBu[:, n % 2], du[:, b % 2],
                        Brep[:, b % 2, n * L:(n + 1) * L].unsqueeze(1).to_broadcast([P, H, L]), ALU.mult).then_inc(dBu_done.sem, 1)
                if (b := batch("x1")) is not None:
                    if b == 0:
                        pool.wait_ge(x_in, 16)
                    wait(pool, gated_done, b)
                    wait(pool, x2_done, H * (b - 2) + H - 1)
                    nc.gpsimd.tensor_tensor(x1[:, b % 2], y[:, b % 2], xin[:, b], ALU.add).then_inc(x1_done.sem, 1)
                if (j := unit("m_rstd")) is not None:
                    wait(pool, xn1_done, j - 1)
                    rsqrt(mrstd[:, :], mve[:, :], m_ve, j, None, m_rstd)
                if (j := unit("xn1b")) is not None:
                    if j == 0:
                        pool.wait_ge(late_in, 16)
                    wait(pool, xn1_done, j)
                    wait(pool, ynw_done, j - 2)
                    nc.gpsimd.tensor_tensor(xn1b[:, j % 2], xn1[:, :], cst["proj_b"], ALU.add).then_inc(xn1b_done.sem, 1)
                if (j := unit("gden")) is not None:
                    wait(pool, gexp_done, j)
                    nc.gpsimd.tensor_scalar(gden[:, :], gexp[:, :], 2.0, 2.0, ALU.mult, ALU.add).then_inc(gden_done.sem, 1)
                    wait(pool, gden_done, j)
                    nc.gpsimd.tensor_tensor(w0[:, :], gden[:, :], neg_one[:, :], ALU.pow).then_inc(w0_done.sem, 1)
                    wait(pool, w0_done, j)
                    nc.gpsimd.tensor_tensor(w1[:, :], gexp[:, :], w0[:, :], ALU.mult).then_inc(w1_done.sem, 1)
                    wait(pool, w1_done, j)
                    wait(pool, topf_done, j)
                    nc.gpsimd.tensor_scalar(pick0[:, :], cst["iota"], topf[:, 0:1], w0[:, :], ALU.is_equal, ALU.mult)
                    nc.gpsimd.tensor_scalar(pick1[:, :], cst["iota"], topf[:, 1:2], w1[:, :], ALU.is_equal, ALU.mult).then_inc(pick_done.sem, 1)
                    wait(pool, pick_done, j)
                    wait(pool, eth_done, j - 2)
                    nc.gpsimd.tensor_tensor(whalf[:, j % 2, :], pick0[:, :], pick1[:, :], ALU.add).then_inc(whalf_done.sem, 1)
                if (j := unit("esum", 0)) is not None:
                    wait(pool, eg_done, j, 2)
                    wait(pool, esum_done, j - 1)
                    nc.gpsimd.tensor_tensor(esum[:, :], eg[:, 0], eg[:, 1], ALU.add).then_inc(esum_done.sem, 1)
                for c in range(2, CHUNKS):
                    if (j := unit("esum", c - 1)) is None:
                        continue
                    wait(pool, eg_done, j, c + 1)
                    wait(pool, esum_done, j, c - 1)
                    nc.gpsimd.tensor_tensor(esum[:, :], esum[:, :], eg[:, c], ALU.add).then_inc(esum_done.sem, 1)
                if (j := unit("comb")) is not None:
                    wait(pool, esum_done, j, 3)
                    wait(pool, combT_mm, j - 1)
                    nc.gpsimd.tensor_tensor(comb[:, :], esum[:, 0:D], esum[:, D:], ALU.add).then_inc(esum_done.sem, 1)
                if (j := unit("yrms")) is not None:
                    wait(pool, ynw_done, j - 1)
                    rsqrt(yrms[:, :], yve[:, :], yve_done, j, None, yrms_done)
                if (j := unit("a_rstd")) is not None:
                    wait(pool, xn2_done, j - 1)
                    rsqrt(arstd[:, :], ave[:, :], a_ve, j, None, a_rstd)
                if (j := unit("b_rstd")) is not None:
                    wait(pool, xn3_done, j - 1)
                    rsqrt(brstd[:, :], bve[:, :], b_ve, j, None, b_rstd)

            pool.wait_ge(zeroed, 1)
            run("pool", slot)

        @block.scalar
        def _(act):
            fn = nc.scalar.activation
            act.wait_ge(early_in, 16)
            fn(negA[:, :], cst["A_log"], ACT.Exp).then_inc(const_a, 1)
            act.wait_ge(const_v, 1)

            def slot(batch, unit):
                if (b := batch("uth")) is not None:
                    wait(act, xc_done, b)
                    wait(act, gate_done, b - 1)
                    for h in range(H):
                        fn(uth[:, h], halves(pP[:, :])[:, h], ACT.Tanh, bias=half_cb[:, h:h + 1], scale=0.5)
                    wait(act, delta_done, b - 1)
                    for h in range(H):
                        i = fn(uhalf[:, h], halves(pP[:, :])[:, h], ACT.Identity, bias=half_cb[:, h:h + 1], scale=0.5)
                    i.then_inc(uhalf_done.sem, 1)
                if (b := batch("dtB")) is not None:
                    wait(act, C_mm, b)
                    wait(act, B_out, b - 1)
                    wait(act, dt_mm, b - 1)
                    fn(dtB[:, :], pP[0:DR + DS, 0:L], ACT.Copy).then_inc(dtB_done.sem, 1)
                if (b := batch("C")) is not None:
                    wait(act, C_mm, b)
                    wait(act, y_done, b - 2)
                    fn(Ct[:, b % 2], pP[:, L:L + H * DS].rearrange("p (h n) -> p h n", h=H), ACT.Copy).then_inc(C_done.sem, 1)
                if (b := batch("sp_abs")) is not None:
                    wait(act, dt_mm, b)
                    wait(act, delta_done, b - 1)
                    for h in range(H):
                        i = fn(sp_abs[:, h], halves(pP[:, :])[:, h], ACT.Abs, bias=cst["dt_b"][:, h:h + 1])
                    i.then_inc(sp_abs_done.sem, 1)
                if (b := batch("sp_pos")) is not None:
                    wait(act, dt_mm, b)
                    wait(act, delta_done, b - 1)
                    wait(act, u_done, b)
                    for h in range(H):
                        i = fn(sp_pos[:, h], halves(pP[:, :])[:, h], ACT.Relu, bias=cst["dt_b"][:, h:h + 1])
                    i.then_inc(sp_pos_done.sem, 1)
                if (b := batch("sp_exp")) is not None:
                    wait(act, sp_abs_done, b)
                    fn(sp_exp[:, :, :], sp_abs[:, :, :], ACT.Exp, scale=-1.0).then_inc(sp_exp_done.sem, 1)
                if (b := batch("sp_log")) is not None:
                    wait(act, sp_exp_done, b)
                    fn(sp_log[:, :, :], sp_exp[:, :, :], ACT.Ln, bias=1.0).then_inc(sp_log_done.sem, 1)
                if (b := batch("y_init")) is not None:
                    wait(act, skip_mm, b)
                    wait(act, x1_done, b - 2)
                    fn(y[:, b % 2], halves(pP[:, :]), ACT.Copy).then_inc(y_init.sem, 1)
                if (b := batch("zth")) is not None:
                    wait(act, zT_done, b)
                    wait(act, u_done, b)
                    fn(zth[:, :, :], halves(pP[:, :]), ACT.Tanh, scale=0.5).then_inc(zth_done.sem, 1)
                if (b := batch("q")) is not None:
                    wait(act, q_mm, b)
                    wait(act, en_mm, b - 1)
                    fn(qT[:, :], pP[:, 0:L], ACT.Identity, bias=cst["bq"]).then_inc(q_done.sem, 1)
                    fn(kT[:, :], pP[:, L:2 * L], ACT.Identity, bias=cst["bk"]).then_inc(k_done.sem, 1)
                if (b := batch("aexp")) is not None:
                    wait(act, amax_done, b)
                    wait(act, attT_mm, b - 1)
                    for h in range(H):
                        i = fn(aexp[:, h], halves(pP[:, :])[:, h], ACT.Exp, bias=amax[:, h:h + 1], accum_out=asum[:, h:h + 1])
                    i.then_inc(aexp_done.sem, 1)
                if (b := batch("att")) is not None:
                    wait(act, aexp_done, b)
                    wait(act, arec_done, b)
                    for h in range(H):
                        i = fn(att[:, h], aexp[:, h], ACT.Identity, scale=arec[:, h:h + 1])
                    i.then_inc(att_done.sem, 1)
                if (b := batch("attT")) is not None:
                    wait(act, attT_mm, b)
                    wait(act, xm_mm, H * (b - 3) + H - 1)
                    fn(attT[:, b % 3], halves(pP[:, :]), ACT.Copy).then_inc(attT_done.sem, 1)
                for n in range(DS):
                    if (b := batch("dA", n)) is None:
                        continue
                    if n == 0:
                        wait(act, delta_done, b)
                    if n >= 2:
                        wait(act, h_done, b, n - 1)
                    else:
                        wait(act, h_done, b - 1, DS - 1 + n)
                    for h in range(H):
                        i = fn(halves(dA[n % 2][:, :])[:, h, 1:], delta[:, b % 2, h, 1:], ACT.Exp,
                               scale=negA_n[:, h * DS + n:h * DS + n + 1])
                    i.then_inc(dA_done.sem, 1)

                def silu_part(j, c):
                    wait(act, expert_mm, j, c + 1)
                    wait(act, esum_done, j - 1)
                    fn(eth[:, c], hE[(c + 1) % 2][:, :], ACT.Tanh, scale=0.5).then_inc(eth_done.sem, 1)
                    wait(act, eth_done, j, 2 * c + 1)
                    wait(act, whalf_done, j)
                    for k in range(2):
                        w = whalf[:, j % 2, 2 * c + k:2 * c + k + 1]
                        i = fn(eth[:, c, k * D:(k + 1) * D], eth[:, c, k * D:(k + 1) * D], ACT.Identity, scale=w, bias=w)
                    i.then_inc(eth_done.sem, 1)

                if (j := unit("xh")) is not None:
                    wait(act, xn1T_mm, j)
                    wait(act, expert_mm, j - 1)
                    fn(xh[:, :, :], halves(hE[0][:, 0:D]), ACT.Copy).then_inc(xh_done.sem, 1)
                if (j := unit("gexp")) is not None:
                    wait(act, gap_done, j)
                    wait(act, w1_done, j - 1)
                    fn(gexp[:, :], gap[:, :], ACT.Exp).then_inc(gexp_done.sem, 1)
                for c in range(CHUNKS):
                    if (j := unit("silu", c)) is not None:
                        silu_part(j, c)
                if (j := unit("combT")) is not None:
                    wait(act, combT_mm, j)
                    wait(act, proj_mm, j - 1)
                    fn(combT[:, :, :], halves(bank_a(j)[:, 0:D]), ACT.Copy).then_inc(combT_done.sem, 1)
                if (j := unit("yss")) is not None:
                    wait(act, yv_done, j)
                    wait(act, yve_done, j - 1)
                    wait(act, yss_done, j - 1)
                    fn(ysq[:, :], xn1b[:, j % 2], ACT.Square, accum_out=yss[:, :]).then_inc(yss_done.sem, 1)
                if (j := unit("xn2T")) is not None:
                    wait(act, xn2T_mm, j)
                    wait(act, xm_mm, j - 1)
                    fn(xn2T[:, :, :], halves(bank_a(j)[:, 0:D]), ACT.Copy).then_inc(xn2T_done.sem, 1)
                if (j := unit("xn3T")) is not None:
                    wait(act, xn3T_mm, j)
                    wait(act, vx_mm, j - 1)
                    wait(act, h1_mm, j - 1)
                    fn(xn3T[:, :, :], halves(bank_b(j)[:, 0:D]), ACT.Copy).then_inc(xn3T_done.sem, 1)
                if (j := unit("h1")) is not None:
                    wait(act, h1_mm, j)
                    wait(act, lg2_mm, j - 1)
                    for h in range(H):
                        i = fn(h1[:, h], halves(bank_b(j)[:, D:])[:, h], ACT.Relu, bias=cst["b1"][:, h:h + 1])
                    i.then_inc(h1_done.sem, 1)
                if (j := unit("alpha")) is not None:
                    wait(act, lmax_done, j)
                    wait(act, avx_done, j - 1)
                    wait(act, lrec_done, j - 1)
                    fn(alpha[:, :], lg2[:, :], ACT.Exp, bias=lmax[:, :], accum_out=lsum[:, :]).then_inc(alpha_done.sem, 1)
                if (j := unit("avxT")) is not None:
                    wait(act, avxT_mm, j)
                    wait(act, o_mm, j - 1)
                    fn(avxT[:, :, :], bank_b(j)[:, :].rearrange("p (k c) -> p k c", k=KT), ACT.Copy).then_inc(avxT_done.sem, 1)

            run("act", slot)

        @block.vector
        def _(dve):
            v = nc.vector

            def x1_of(j):
                return x1[:, j // H % 2, j % H]

            for bank in dA:
                v.memset(halves(bank[:, :])[:, :, 0:1], 0.0)
            v.memset(warm[:, :], 0.0).then_inc(warm_ready, 1)
            dve.wait_ge(early_in, 16)
            for h in range(H):
                cols = slice(h * P, (h + 1) * P)
                v.tensor_tensor(convW[:, :, cols], convW[:, :, cols],
                                cst["in_projT"][:, cols].unsqueeze(1).to_broadcast([P, DC, P]), ALU.mult).then_inc(conv_ready, 1)
            v.tensor_scalar(half_cb[:, :], cst["conv_b"], 0.5, None, ALU.mult)
            for h in range(H):
                v.tensor_scalar(diagD[:, h], ident, cst["Dskip"][:, h:h + 1], None, ALU.mult)
            dve.wait_ge(const_a, 1)
            v.tensor_scalar(negA_n[:, :], negA[:, :], -1.0, None, ALU.mult).then_inc(const_v, 1)

            def expert_piece(t, k):
                n = H * E * D // PIECES
                return t[:, k * n:(k + 1) * n]

            def split_small():
                dve.wait_ge(late_in, 16)
                dve.wait_ge(expert_b_in, 16)
                dve.wait_ge(zeroed, 1)
                v.tensor_copy(ones2r[:, :], ones2[:, :])
                router = halves(cst["router"])
                v.tensor_copy(rw_hi[:, :, :], router).then_inc(router_split, 1)
                v.tensor_copy(eb_hi[:, :], eb_raw[:, :]).then_inc(bias_split, 1)
                dve.wait_ge(router_split, 1)
                v.tensor_tensor(rw_lo[:, :, :], router, rw_hi[:, :, :].bitcast(F32), ALU.subtract).then_inc(router_split, 1)
                dve.wait_ge(bias_split, 1)
                v.tensor_tensor(eb_lo[:, :], eb_raw[:, :], eb_hi[:, :].bitcast(F32), ALU.subtract).then_inc(bias_split, 1)

            def aggregate(mv, st, s_stats, s_mv, j):
                wait(dve, s_stats, j)
                v.bn_aggr(mv[:, :], st[:, :]).then_inc(s_mv.sem, 1)

            def add_eps(ve, mv, s_mv, s_ve, j):
                wait(dve, s_mv, j)
                v.tensor_scalar(ve[:, :], mv[:, 1:2], 1e-5, None, ALU.add).then_inc(s_ve.sem, 1)

            def normalize_unit(dst, src, mv, rstd, s_rstd, j, done):
                wait(dve, s_rstd, j)
                v.tensor_scalar(dst, src, mv[:, 0:1], rstd[:, :], ALU.subtract, ALU.mult).then_inc(done.sem, 1)

            def weighted_silu(j, c):
                wait(dve, eth_done, j, 2 * c + 2)
                v.tensor_tensor(eg[:, c], hE[(c + 1) % 2][:, :], eth[:, c], ALU.mult).then_inc(eg_done.sem, 1)

            def stats(src, st, mv, ve, eps, s_stats, s_mv, s_ve, b, k):
                for h in range(H):
                    i = v.bn_stats(st[:, h], src[:, h])
                i.then_inc(s_stats.sem, 1)
                wait(dve, s_stats, b, k)
                for h in range(H):
                    i = v.bn_aggr(mv[:, h], st[:, h])
                i.then_inc(s_mv.sem, 1)
                wait(dve, s_mv, b, k)
                v.tensor_scalar(ve, mv[:, :, 1], eps, None, ALU.add).then_inc(s_ve.sem, 1)

            def normalize(dst, src, mv, rstd, s_rstd, b, k, done):
                wait(dve, s_rstd, b, k)
                for h in range(H):
                    i = v.tensor_scalar(dst[:, h], src[:, h], mv[:, h, 0:1], rstd[:, h:h + 1], ALU.subtract, ALU.mult)
                i.then_inc(done.sem, 1)

            def slot(batch, unit):
                if (b := batch("g_stats")) is not None:
                    if b == 0:
                        dve.wait_ge(x_in, 16)
                    stats(xin[:, b], gst, gmv, gve[:, :], 1e-5, g_stats, g_mv, g_ve, b, None)
                if (b := batch("u")) is not None:
                    wait(dve, uhalf_done, b)
                    wait(dve, du_done, b - 1)
                    wait(dve, skip_mm, b - 1)
                    v.scalar_tensor_tensor(u[:, :, :], uth[:, :, :], 1.0, uhalf[:, :, :], ALU.add, ALU.mult).then_inc(u_done.sem, 1)
                if (b := batch("zn")) is not None:
                    wait(dve, zT_done, b - 1)
                    normalize(zn, xin[:, b], gmv, grstd, g_rstd, b, None, zn_done)
                if (b := batch("delta")) is not None:
                    wait(dve, sp_pos_done, b)
                    wait(dve, sp_log_done, b)
                    wait(dve, dA_done, b - 2)
                    v.tensor_tensor(delta[:, b % 2], sp_pos[:, :, :], sp_log[:, :, :], ALU.add).then_inc(delta_done.sem, 1)
                if (b := batch("gate")) is not None:
                    wait(dve, zth_done, b)
                    wait(dve, gated_done, b - 2)
                    v.scalar_tensor_tensor(gate[:, b % 2], zth[:, :, :], 1.0, halves(pP[:, :]), ALU.add, ALU.mult).then_inc(gate_done.sem, 1)
                if (b := batch("split_small")) is not None and b == 0:
                    split_small()
                for k in range(PIECES):
                    if batch("experts_hi", k) == 0:
                        dve.wait_ge(experts_in, 16)
                        v.tensor_copy(expert_piece(ew_hi_r, k), expert_piece(ew_raw, k)).then_inc(experts_hi, 1)
                for k in range(PIECES):
                    if batch("experts_lo", k) == 0:
                        dve.wait_ge(experts_hi, k + 1)
                        v.tensor_tensor(expert_piece(ew_lo_r, k), expert_piece(ew_raw, k),
                                        expert_piece(ew_hi_r, k).bitcast(F32), ALU.subtract).then_inc(experts_split, 1)
                if (b := batch("amax")) is not None:
                    wait(dve, en_mm, b)
                    wait(dve, aexp_done, b - 1)
                    v.tensor_reduce(amax[:, :], halves(pP[:, :]), AX.X, ALU.max, negate=True).then_inc(amax_done.sem, 1)
                if (b := batch("arec")) is not None:
                    wait(dve, aexp_done, b)
                    wait(dve, att_done, b - 1)
                    v.reciprocal(arec[:, :], asum[:, :]).then_inc(arec_done.sem, 1)
                for n in range(DS):
                    if (b := batch("scan", n)) is None:
                        continue
                    wait(dve, dA_done, b, n + 1)
                    wait(dve, dBu_done, b, n + 1)
                    if n >= 2:
                        wait(dve, hT_done, b, n - 1)
                    else:
                        wait(dve, hT_done, b - 1, DS - 1 + n)
                    v.tensor_tensor_scan(out=hst[:, n % 2].rearrange("p h l -> p (h l)"), data0=dA[n % 2][:, :],
                                         data1=dBu[:, n % 2].rearrange("p h l -> p (h l)"), initial=0.0,
                                         op0=ALU.mult, op1=ALU.add).then_inc(h_done.sem, 1)
                for n in range(DS):
                    if (b := batch("y", n)) is None:
                        continue
                    if n == 0:
                        wait(dve, y_init, b)
                        wait(dve, C_done, b)
                    wait(dve, hT_done, b, n + 1)
                    for h in range(H):
                        if n:
                            wait(dve, y_done, b, H * (n - 1) + h + 1)
                        v.scalar_tensor_tensor(y[:, b % 2, h], halves(hT[:, :])[:, h], Ct[:, b % 2, h, n:n + 1],
                                               y[:, b % 2, h], ALU.mult, ALU.add).then_inc(y_done.sem, 1)
                if (b := batch("gated")) is not None:
                    wait(dve, y_done, b)
                    wait(dve, gate_done, b)
                    v.scalar_tensor_tensor(y[:, b % 2], y[:, b % 2], 0.5, gate[:, b % 2], ALU.mult, ALU.mult).then_inc(gated_done.sem, 1)
                if (j := unit("m_stats")) is not None:
                    wait(dve, x1_done, j // H)
                    v.bn_stats(mst[:, :], x1_of(j)).then_inc(m_stats.sem, 1)
                if (j := unit("m_mv")) is not None:
                    aggregate(mmv, mst, m_stats, m_mv, j)
                if (j := unit("m_ve")) is not None:
                    add_eps(mve, mmv, m_mv, m_ve, j)
                if (j := unit("xn1")) is not None:
                    wait(dve, xn1b_done, j - 1)
                    wait(dve, xn1T_mm, j - 1)
                    normalize_unit(xn1[:, :], x1_of(j), mmv, mrstd, m_rstd, j, xn1_done)
                if (j := unit("xl")) is not None:
                    wait(dve, xh_done, j)
                    v.tensor_tensor(xl[:, :, :], halves(hE[0][:, 0:D]), xh[:, :, :].bitcast(F32), ALU.subtract).then_inc(xl_done.sem, 1)
                if (j := unit("logit")) is not None:
                    wait(dve, logit_mm, j)
                    v.tensor_tensor(logit[:, :], hE[0][:, D:D + E], cst["router_b"], ALU.add).then_inc(logit_done.sem, 1)
                if (j := unit("top")) is not None:
                    wait(dve, logit_done, j)
                    v.max(top[:, :], logit[:, :]).then_inc(top_done.sem, 1)
                if (j := unit("gap")) is not None:
                    wait(dve, top_done, j)
                    v.tensor_tensor(gap[:, :], top[:, 1:2], top[:, 0:1], ALU.subtract).then_inc(gap_done.sem, 1)
                    v.max_index(topi[:, :], top[:, :], logit[:, :]).then_inc(topi_done.sem, 1)
                if (j := unit("topf")) is not None:
                    wait(dve, topi_done, j)
                    wait(dve, whalf_done, j - 1)
                    v.tensor_copy(topf[:, :], topi[:, :]).then_inc(topf_done.sem, 1)
                for c in range(CHUNKS):
                    if (j := unit("eg", c)) is not None:
                        weighted_silu(j, c)
                if (j := unit("yv")) is not None:
                    wait(dve, proj_mm, j)
                    wait(dve, xn1b_done, j)
                    v.tensor_tensor(xn1b[:, j % 2], bank_a(j)[:, D:], xn1b[:, j % 2], ALU.add).then_inc(yv_done.sem, 1)
                if (j := unit("yve")) is not None:
                    wait(dve, yss_done, j)
                    wait(dve, yrms_done, j - 1)
                    v.tensor_scalar(yve[:, :], yss[:, :], 1.0 / D, 1e-6, ALU.mult, ALU.add).then_inc(yve_done.sem, 1)
                if (j := unit("ynw")) is not None:
                    wait(dve, yrms_done, j)
                    v.scalar_tensor_tensor(ynw[:, :], xn1b[:, j % 2], yrms[:, :], cst["norm_w"], ALU.mult, ALU.mult).then_inc(ynw_done.sem, 1)
                if (j := unit("x2")) is not None:
                    wait(dve, ynw_done, j)
                    wait(dve, x3_done, j - 1)
                    v.tensor_tensor(x2[:, :], ynw[:, :], x1_of(j), ALU.add).then_inc(x2_done.sem, 1)
                if (j := unit("a_stats")) is not None:
                    wait(dve, x2_done, j)
                    v.bn_stats(ast[:, :], x2[:, :]).then_inc(a_stats.sem, 1)
                if (j := unit("a_mv")) is not None:
                    aggregate(amv, ast, a_stats, a_mv, j)
                if (j := unit("a_ve")) is not None:
                    add_eps(ave, amv, a_mv, a_ve, j)
                if (j := unit("xn2")) is not None:
                    wait(dve, xn2T_mm, j - 1)
                    normalize_unit(xn2[:, :], x2[:, :], amv, arstd, a_rstd, j, xn2_done)
                if (j := unit("x3")) is not None:
                    wait(dve, xm_mm, j)
                    wait(dve, xout_done, j - 2)
                    v.tensor_tensor(x3[:, j % 2], bank_a(j)[:, D:], x2[:, :], ALU.add).then_inc(x3_done.sem, 1)
                if (j := unit("b_stats")) is not None:
                    wait(dve, x3_done, j)
                    v.bn_stats(bst[:, :], x3[:, j % 2]).then_inc(b_stats.sem, 1)
                if (j := unit("b_mv")) is not None:
                    aggregate(bmv, bst, b_stats, b_mv, j)
                if (j := unit("b_ve")) is not None:
                    add_eps(bve, bmv, b_mv, b_ve, j)
                if (j := unit("xn3")) is not None:
                    wait(dve, xn3T_mm, j - 1)
                    normalize_unit(xn3[:, :], x3[:, j % 2], bmv, brstd, b_rstd, j, xn3_done)
                if (j := unit("lg2")) is not None:
                    wait(dve, lg2_mm, j)
                    wait(dve, alpha_done, j - 1)
                    v.tensor_tensor(lg2[:, :], bank_b(j)[:, 0:K], cst["b2"], ALU.add).then_inc(lg2_done.sem, 1)
                if (j := unit("lmax")) is not None:
                    wait(dve, lg2_done, j)
                    v.tensor_reduce(lmax[:, :], lg2[:, :], AX.X, ALU.max, negate=True).then_inc(lmax_done.sem, 1)
                if (j := unit("avx")) is not None:
                    wait(dve, vx_mm, j)
                    wait(dve, alpha_done, j)
                    wait(dve, avxT_mm, j - 1)
                    v.tensor_tensor(avx[:, :, :], bank_vx(j)[:, :].rearrange("p (k r) -> p k r", k=K),
                                    alpha[:, :].unsqueeze(2).to_broadcast([P, K, R]), ALU.mult).then_inc(avx_done.sem, 1)
                if (j := unit("lrec")) is not None:
                    wait(dve, alpha_done, j)
                    wait(dve, xout_done, j - 1)
                    v.reciprocal(lrec[:, :], lsum[:, :]).then_inc(lrec_done.sem, 1)
                if (j := unit("xout")) is not None:
                    wait(dve, o_mm, j)
                    wait(dve, lrec_done, j)
                    wait(dve, stored[j % 2], j // 2 - 1)
                    v.scalar_tensor_tensor(xout[:, j % 2], bank_b(j)[:, 0:D], lrec[:, :], x3[:, j % 2], ALU.mult, ALU.add).then_inc(xout_done.sem, 1)

            run("dve", slot)

        @block.tensor
        def _(pe):
            def mm(out_, lhsT, rhs, first, last, **kw):
                return nc.tensor.matmul(out_, lhsT, rhs, start=first, stop=last, **kw)

            def transposes(dst, src):
                for j in range(H):
                    for i in range(H):
                        last = nc.tensor.transpose(halves(dst)[:, j, i * P:(i + 1) * P], src[:, i, j * P:(j + 1) * P], ident)
                return last

            pe.wait_ge(warm_ready, 1)
            for _ in range(WARM_UP):
                mm(pB[:, 0:L], warm[:, 0:P], warm[:, :], True, True)

            def slot(batch, unit):
                if (b := batch("xc")) is not None:
                    if b == 0:
                        pe.wait_ge(ctx_in, 16)
                        pe.wait_ge(zeroed, 1)
                    wait(pe, gate_done, b - 1)
                    wait(pe, attT_done, b - 2)
                    for h in range(H):
                        if b == 0:
                            pe.wait_ge(conv_ready, h + 1)
                        for j in range(DC):
                            i = mm(halves(pP[:, :])[:, h], convW[:, j, h * P:(h + 1) * P], ctx[:, b, j:j + L], j == 0, j == DC - 1)
                    i.then_inc(xc_done.sem, 1)
                if (b := batch("dtB")) is not None:
                    wait(pe, u_done, b)
                    for h in range(H):
                        i = mm(pP[0:DR + DS, 0:L], xproj[:, h, 0:DR + DS], u[:, h], h == 0, h == H - 1)
                    i.then_inc(dtB_mm.sem, 1)
                    for g in range(H):
                        for h in range(H):
                            i = mm(pP[:, L + g * DS:L + (g + 1) * DS], u[:, h, g * P:(g + 1) * P], xproj[:, h, DR + DS:], h == 0, h == H - 1)
                    i.then_inc(C_mm.sem, 1)
                if (b := batch("dt")) is not None:
                    if b == 0:
                        pe.wait_ge(dtp_in, 16)
                    wait(pe, dtB_done, b)
                    wait(pe, C_done, b)
                    for h in range(H):
                        i = mm(halves(pP[:, :])[:, h], dtp[:, h * P:(h + 1) * P], dtB[0:DR, :], True, True)
                    i.then_inc(dt_mm.sem, 1)
                if (b := batch("skip")) is not None:
                    if b == 0:
                        pe.wait_ge(const_v, 1)
                    wait(pe, sp_abs_done, b)
                    wait(pe, sp_pos_done, b)
                    for g in range(H):
                        for h in range(H):
                            i = mm(halves(pP[:, :])[:, g, h * P:(h + 1) * P], u[:, h, g * P:(g + 1) * P], diagD[:, h], True, True)
                    i.then_inc(skip_mm.sem, 1)
                if (b := batch("zT")) is not None:
                    wait(pe, y_init, b)
                    wait(pe, zn_done, b)
                    transposes(pP[:, :], zn).then_inc(zT_done.sem, 1)
                if (b := batch("q")) is not None:
                    if b == 0:
                        pe.wait_ge(late_in, 16)
                    wait(pe, gate_done, min(b + 1, B - 1))
                    wait(pe, attT_done, b - 1)
                    mm(pP[:, 0:L], cst["WqT"], ctx[:, b, DC - 1:], True, True)
                    mm(pP[:, L:2 * L], cst["WkT"], ctx[:, b, DC - 1:], True, True).then_inc(q_mm.sem, 1)
                if (b := batch("en")) is not None:
                    wait(pe, q_done, b)
                    wait(pe, k_done, b)
                    for h in range(H):
                        i = mm(halves(pP[:, :])[:, h], qT[:, h * P:(h + 1) * P], kT[:, :], True, True)
                    i.then_inc(en_mm.sem, 1)
                if (b := batch("attT")) is not None:
                    wait(pe, att_done, b)
                    transposes(pP[:, :], att).then_inc(attT_mm.sem, 1)
                for n in range(DS):
                    if (b := batch("hT", n)) is None:
                        continue
                    wait(pe, h_done, b, n + 1)
                    wait(pe, y_done, b if n else b - 1, H * n if n else None)
                    transposes(hT[:, :], hst[:, n % 2]).then_inc(hT_done.sem, 1)

                def transposes_unit(dst, src):
                    for h in range(src.shape[-1] // P):
                        last = nc.tensor.transpose(dst[:, h * P:(h + 1) * P], src[:, h * P:(h + 1) * P], ident)
                    return last

                if (j := unit("xn1T")) is not None:
                    wait(pe, xn1_done, j)
                    wait(pe, eg_done, j - 1)
                    transposes_unit(hE[0], xn1).then_inc(xn1T_mm.sem, 1)
                if (j := unit("logit")) is not None:
                    if j == 0:
                        pe.wait_ge(router_split, 2)
                    wait(pe, xl_done, j)
                    n = 0
                    for h in range(H):
                        for a, w in ((xh, rw_hi), (xl, rw_hi), (xh, rw_lo)):
                            i = mm(hE[0][:, D:D + E], a[:, h], w[:, h], n == 0, n == 3 * H - 1)
                            n += 1
                    i.then_inc(logit_mm.sem, 1)
                for c in range(CHUNKS):
                    if (j := unit("expert", c)) is None:
                        continue
                    if c == 0:
                        if j == 0:
                            pe.wait_ge(experts_split, PIECES)
                            pe.wait_ge(eb_rows_in, 32)
                        wait(pe, xl_done, j)
                        wait(pe, eg_done, j - 1, CHUNKS - 1)
                    if c == 1:
                        wait(pe, logit_done, j)
                    if c >= 2:
                        wait(pe, eg_done, j, c - 1)
                    cols = slice(c * 2 * D, (c + 1) * 2 * D)
                    bank = hE[(c + 1) % 2]
                    for h in range(H):
                        for n, (a, w) in enumerate(((xh, ew_hi), (xl, ew_hi), (xh, ew_lo))):
                            mm(bank[:, :], a[:, h], w[:, h, cols], h == 0 and n == 0, False)
                    mm(bank[:, :], ones2r[:, :], eb_rows[:, cols], False, True).then_inc(expert_mm.sem, 1)
                if (j := unit("combT")) is not None:
                    wait(pe, esum_done, j)
                    wait(pe, x3_done, j - 1 if j <= FREED else j - 2)
                    if bank_a(j) is pP:
                        wait(pe, attT_done, B - 1)
                    transposes_unit(bank_a(j), comb).then_inc(combT_mm.sem, 1)
                if (j := unit("proj")) is not None:
                    wait(pe, combT_done, j)
                    for h in range(H):
                        i = mm(bank_a(j)[:, D:], combT[:, h], halves(cst["proj"])[:, h], h == 0, h == H - 1)
                    i.then_inc(proj_mm.sem, 1)
                if (j := unit("xn2T")) is not None:
                    wait(pe, xn2_done, j)
                    wait(pe, yv_done, j)
                    transposes_unit(bank_a(j), xn2).then_inc(xn2T_mm.sem, 1)
                if (j := unit("xm")) is not None:
                    wait(pe, xn2T_done, j)
                    wait(pe, attT_done, j // H)
                    for h in range(H):
                        i = mm(bank_a(j)[:, D:], xn2T[:, h], attT[:, j // H % 3, h], h == 0, h == H - 1)
                    i.then_inc(xm_mm.sem, 1)
                if (j := unit("xn3T")) is not None:
                    wait(pe, xn3_done, j)
                    wait(pe, xout_done, j - 1 if j <= FREED else j - 2)
                    if bank_b(j) is dA[1]:
                        wait(pe, h_done, B - 1)
                    transposes_unit(bank_b(j), xn3).then_inc(xn3T_mm.sem, 1)
                if (j := unit("h1")) is not None:
                    wait(pe, xn3T_done, j)
                    w1v = halves(cst["W1"])
                    for g in range(H):
                        for h in range(H):
                            i = mm(halves(bank_b(j)[:, D:])[:, g], w1v[:, h, g * P:(g + 1) * P], xn3T[:, h], h == 0, h == H - 1)
                    i.then_inc(h1_mm.sem, 1)
                if (j := unit("lg2")) is not None:
                    wait(pe, h1_done, j)
                    for h in range(H):
                        i = mm(bank_b(j)[:, 0:K], h1[:, h], halves(cst["W2"])[:, h], h == 0, h == H - 1)
                    i.then_inc(lg2_mm.sem, 1)
                if (j := unit("vx")) is not None:
                    if j < FREED:
                        wait(pe, lg2_done, j)
                    else:
                        wait(pe, h_done, B - 1)
                        wait(pe, xn3T_done, j)
                        wait(pe, avx_done, j - 1)
                    for h in range(H):
                        i = mm(bank_vx(j)[:, :], xn3T[:, h], halves(cst["VT"])[:, h], h == 0, h == H - 1)
                    i.then_inc(vx_mm.sem, 1)
                if (j := unit("avxT")) is not None:
                    wait(pe, avx_done, j)
                    transposes_unit(bank_b(j), avx[:, :, :].rearrange("p k r -> p (k r)")).then_inc(avxT_mm.sem, 1)
                if (j := unit("o")) is not None:
                    wait(pe, avxT_done, j)
                    ut = cst["UT"].rearrange("p (k d) -> p k d", k=KT)
                    for k in range(KT):
                        i = mm(bank_b(j)[:, 0:D], avxT[:, k], ut[:, k], k == 0, k == KT - 1)
                    i.then_inc(o_mm.sem, 1)

            run("pe", slot)


def kernel(**inputs):
    import numpy as np
    import concourse.bacc as bacc
    from concourse.bass_utils import run_bass_kernel_spmd

    a = {k: np.asarray(v) for k, v in inputs.items()}

    def halves(m):
        return m.reshape(-1, P, m.shape[1]).transpose(1, 0, 2).reshape(P, -1)

    def everywhere(row):
        return np.broadcast_to(row.reshape(1, -1), (P, row.size))

    laid = {
        "in_projT": a["L0_xattn_in_proj_w"].T, "conv_w": everywhere(a["L0_xattn_conv_w"].T),
        "conv_b": halves(a["L0_xattn_conv_b"][:, None]), "x_projT": halves(a["L0_xattn_x_proj_w"].T),
        "dt_b": halves(a["L0_xattn_dt_proj_b"][:, None]), "Dskip": halves(a["L0_xattn_D"][:, None]),
        "A_log": halves(a["L0_xattn_A_log"]), "ident": np.eye(P, dtype=np.float32),
        "WqT": a["L1_xattn_Wq"].T, "WkT": a["L1_xattn_Wk"].T, "bq": a["L1_xattn_bq"][:, None], "bk": a["L1_xattn_bk"][:, None],
        "router": halves(a["L0_ffn_router_w"]), "router_b": everywhere(a["L0_ffn_router_b"]),
        "proj": halves(a["L0_ffn_proj_w"]), "proj_b": everywhere(a["L0_ffn_proj_b"]), "norm_w": everywhere(a["L0_ffn_norm_w"]),
        "W1": halves(a["L1_ffn_W1"]), "b1": halves(a["L1_ffn_b1"][:, None]), "W2": halves(a["L1_ffn_W2"]),
        "b2": everywhere(a["L1_ffn_b2"]), "VT": halves(a["L1_ffn_V"].reshape(K * R, D).T),
        "UT": halves(a["L1_ffn_U"].transpose(0, 2, 1).reshape(K * R, D)), "iota": everywhere(np.arange(E, dtype=np.float32)),
    }
    arrays = {
        "early": np.concatenate([laid[n] for n, _ in EARLY], axis=1),
        "late": np.concatenate([laid[n] for n, _ in LATE], axis=1),
        "experts": halves(a["L0_ffn_expert_w"].transpose(1, 0, 2).reshape(D, E * D)),
        "expert_b": a["L0_ffn_expert_b"].reshape(P, -1),
        "dt_projT": a["L0_xattn_dt_proj_w"].T,
        "ctxT": a["ctx_1024"].transpose(2, 0, 1),
        "x": a["x"].reshape(B, H, P, D).transpose(2, 0, 1, 3),
    }
    arrays = {k: np.ascontiguousarray(m) for k, m in arrays.items()}
    nc = bacc.Bacc("TRN2", target_bir_lowering=False, num_devices=1)
    args = [nc.dram_tensor(k, m.shape, mybir.dt.from_np(m.dtype), kind="ExternalInput").ap() for k, m in arrays.items()]
    out = nc.dram_tensor("out", (P, B, H, D), F32, kind="ExternalOutput").ap()
    build(nc, *args, out)
    got = run_bass_kernel_spmd(nc, [arrays], core_ids=[0]).results[0]["out"]
    return np.ascontiguousarray(got.transpose(1, 2, 0, 3)).reshape(B, L, D)
```
